# Optimizing a Trainium2 kernel written in Bass

```python
import numpy as np
import jax
import jax.numpy as jnp

def _softmax(x, axis=-1):
    return jax.nn.softmax(x, axis=axis)
def _gelu(x):
    return jax.nn.gelu(x, approximate=True)
def _silu(x):
    return jax.nn.silu(x)
def _sigmoid(x):
    return jax.nn.sigmoid(x)
def _layernorm(x, axis=-1, eps=1e-5):
    m = jnp.mean(x, axis=axis, keepdims=True)
    v = jnp.var(x, axis=axis, keepdims=True)
    return (x - m) / jnp.sqrt(v + eps)
def _scatter_add(tgt, idx, src, axis=0):
    return tgt.at[idx].add(src)
def _segment_sum(src, seg, n):
    return jax.ops.segment_sum(src, seg, n)

kernel_name = 'mk_conv_preact_d1_conv_nhwc64_5c4015'

def setup_inputs(seed: int = 0):
    np.random.seed(seed)
    _w = jnp.asarray
    def _rec_inputs():
        import jax
        import jax.numpy as jnp
        _gk = jax.random.key(seed)
        x = -0.0004039 + 1 * jax.random.normal(jax.random.fold_in(_gk, 1), (1, 512, 384, 64), jnp.float32)
        return x
    x = _rec_inputs()
    def _L0_conv_setup():
        import jax, jax.numpy as jnp
        import numpy as np
        INF = 1000000000.0
        EPS = 1e-05

        def layer_norm(x, g, b):
            mu = jnp.mean(x, axis=-1, keepdims=True)
            var = jnp.mean(jnp.square(x - mu), axis=-1, keepdims=True)
            return (x - mu) * jax.lax.rsqrt(var + EPS) * g + b
        key = jax.random.key(seed)
        ks = jax.random.split(key, 12)
        B, S, N = (1, 512, 384)
        c_in, c_hid, c_z, H = (64, 32, 128, 8)
        d = c_hid * H
        sc = lambda fan: 1.0 / np.sqrt(fan)
        return {'m': jax.random.normal(ks[0], (B, S, N, c_in), jnp.float32), 'z': jax.random.normal(ks[1], (B, N, N, c_z), jnp.float32), 'mask': jnp.ones((B, N, N), jnp.float32), 'gamma_m': jnp.ones((c_in,), jnp.float32), 'beta_m': jnp.zeros((c_in,), jnp.float32), 'gamma_z': jnp.ones((c_z,), jnp.float32), 'beta_z': jnp.zeros((c_z,), jnp.float32), 'w_z': jax.random.normal(ks[2], (c_z, H), jnp.float32) * sc(c_z), 'b_z': jnp.zeros((H,), jnp.float32), 'w_v': jax.random.normal(ks[3], (c_in, d), jnp.float32) * sc(c_in), 'b_v': jnp.zeros((d,), jnp.float32), 'w_g': jax.random.normal(ks[4], (c_in, d), jnp.float32) * sc(c_in), 'b_g': jnp.zeros((d,), jnp.float32), 'w_o': jax.random.normal(ks[5], (d, c_in), jnp.float32) * sc(d), 'b_o': jnp.zeros((c_in,), jnp.float32)}
    _L0_conv_all = _L0_conv_setup()
    _L0_conv_in = {k: v for k, v in _L0_conv_all.items() if k in ('z', 'mask', 'gamma_m', 'beta_m', 'gamma_z', 'beta_z', 'w_z', 'b_z', 'w_v', 'b_v', 'w_g', 'b_g', 'w_o', 'b_o', )}
    del _L0_conv_all

    return {
        "x": x,
        "L0_conv_z": _L0_conv_in["z"],
        "L0_conv_mask": _L0_conv_in["mask"],
        "L0_conv_gamma_m": _L0_conv_in["gamma_m"],
        "L0_conv_beta_m": _L0_conv_in["beta_m"],
        "L0_conv_gamma_z": _L0_conv_in["gamma_z"],
        "L0_conv_beta_z": _L0_conv_in["beta_z"],
        "L0_conv_w_z": _L0_conv_in["w_z"],
        "L0_conv_b_z": _L0_conv_in["b_z"],
        "L0_conv_w_v": _L0_conv_in["w_v"],
        "L0_conv_b_v": _L0_conv_in["b_v"],
        "L0_conv_w_g": _L0_conv_in["w_g"],
        "L0_conv_b_g": _L0_conv_in["b_g"],
        "L0_conv_w_o": _L0_conv_in["w_o"],
        "L0_conv_b_o": _L0_conv_in["b_o"],
    }

def reference(x, L0_conv_z, L0_conv_mask, L0_conv_gamma_m, L0_conv_beta_m, L0_conv_gamma_z, L0_conv_beta_z, L0_conv_w_z, L0_conv_b_z, L0_conv_w_v, L0_conv_b_v, L0_conv_w_g, L0_conv_b_g, L0_conv_w_o, L0_conv_b_o):
    import jax
    import jax.numpy as jnp
    def _L0_conv_ref(m, z, mask, gamma_m, beta_m, gamma_z, beta_z, w_z, b_z, w_v, b_v, w_g, b_g, w_o, b_o):
        import jax, jax.numpy as jnp
        import numpy as np
        INF = 1000000000.0
        EPS = 1e-05

        def layer_norm(x, g, b):
            mu = jnp.mean(x, axis=-1, keepdims=True)
            var = jnp.mean(jnp.square(x - mu), axis=-1, keepdims=True)
            return (x - mu) * jax.lax.rsqrt(var + EPS) * g + b
        B, S, N, c_in = m.shape
        H = w_z.shape[-1]
        C = w_v.shape[-1] // H
        zn = layer_norm(z, gamma_z, beta_z)
        logits = jnp.einsum('bqkz,zh->bhqk', zn, w_z) + b_z[None, :, None, None]
        logits = logits + (INF * (mask - 1.0))[:, None, :, :]
        w = jax.nn.softmax(logits, axis=-1)
        mn = layer_norm(m, gamma_m, beta_m)
        v = (mn @ w_v + b_v).reshape(B, S, N, H, C)
        o = jnp.einsum('bhqk,bskhc->bsqhc', w, v)
        g = jax.nn.sigmoid(mn @ w_g + b_g).reshape(B, S, N, H, C)
        out = (o * g).reshape(B, S, N, H * C) @ w_o + b_o
        return out

    def _gn(v, G=32, eps=1e-5):
        B_, H_, W_, C_ = v.shape
        g = v.reshape(B_, H_, W_, G, C_ // G)
        m = jnp.mean(g, axis=(1, 2, 4), keepdims=True)
        s = jnp.var(g, axis=(1, 2, 4), keepdims=True)
        return ((g - m) / jnp.sqrt(s + eps)).reshape(v.shape)

    def _ln_c(v, eps=1e-6):
        m = jnp.mean(v, axis=-1, keepdims=True)
        s = jnp.var(v, axis=-1, keepdims=True)
        return (v - m) / jnp.sqrt(s + eps)

    def _ln_t(v, eps=1e-5):
        m = jnp.mean(v, axis=-1, keepdims=True)
        s = jnp.var(v, axis=-1, keepdims=True)
        return (v - m) / jnp.sqrt(s + eps)

    def _to_tokens(v):
        B_, H_, W_, C_ = v.shape
        return v.reshape(B_, H_ * W_, C_)
    def _from_tokens(t, like):
        return t.reshape(like.shape)

    x = x + _L0_conv_ref(_gn(x), L0_conv_z, L0_conv_mask, L0_conv_gamma_m, L0_conv_beta_m, L0_conv_gamma_z, L0_conv_beta_z, L0_conv_w_z, L0_conv_b_z, L0_conv_w_v, L0_conv_b_v, L0_conv_w_g, L0_conv_b_g, L0_conv_w_o, L0_conv_b_o)
    return x


_drawn_inputs = setup_inputs


def setup_inputs(seed=0):
    import zlib

    import numpy as np

    out = dict(_drawn_inputs(seed))
    spreads = {'L0_conv_gamma_m': (1.0, 0.6),
     'L0_conv_beta_m': (0.0, 0.1),
     'L0_conv_gamma_z': (1.0, 0.6),
     'L0_conv_beta_z': (0.0, 2.0),
     'L0_conv_b_z': (0.0, 2.0),
     'L0_conv_b_v': (0.0, 0.1),
     'L0_conv_b_g': (0.0, 2.0),
     'L0_conv_b_o': (0.0, 0.1)}
    factors = {}
    for name, (base, spread) in spreads.items():
        noise = np.random.default_rng([zlib.crc32(name.encode()), seed]).standard_normal(out[name].shape)
        drawn = base * np.exp(spread * noise) if base else spread * noise
        out[name] = jnp.asarray(drawn.astype(out[name].dtype))
    for name, factor in factors.items():
        out[name] = (out[name] * factor).astype(out[name].dtype)
    return out
```

```python
from contextlib import ExitStack

import concourse.bass as bass
from concourse import mybir

F32 = mybir.dt.float32
F16 = mybir.dt.float16
I32 = mybir.dt.int32
ALU = mybir.AluOpType
ACT = mybir.ActivationFunctionType
AX_X = mybir.AxisListType.X
ABSMAX = bass.bass_isa.ReduceOp.absmax

P = 128
EPS = 1e-5
INF = 1e9
W_SCALE = 2.0 ** 14
W_TARGET = 2.0 ** 7

R = 8
PAIRS = 12
PERIOD = 2 * PAIRS
FIRST = 8
AHEAD = 21


def pair_weighted(nc, x, z, mask, gamma_m, beta_m, gamma_z, beta_z, w_z, b_z, w_v, b_v, w_g, b_g, w_o, b_o, out):
    _, S, N, C = x.shape
    CZ = z.shape[-1]
    H = w_z.shape[-1]
    D = w_v.shape[-1]
    HC = D // H
    T = N // P
    NG = S // R
    STEPS = NG * PAIRS
    LOOPS = (STEPS - AHEAD - FIRST) // PERIOD
    TAIL = FIRST + LOOPS * PERIOD
    assert (T, C, CZ, H, D) == (3, 64, 128, 8, 256)

    ZB = 16
    ITER = 6
    QT_LOOPS = N // (ZB * ITER)
    NB = T * QT_LOOPS * ITER
    XB = 64
    NX = S * N // P // XB
    GRP = 32
    assert NX == 2 * T * QT_LOOPS

    x_rows = x.rearrange("o s (p t) c -> p (o s) (t c)", t=T)
    out_rows = out.rearrange("o s (p t) c -> p (o s) (t c)", t=T)
    x_flat = x.rearrange("o s n c -> (o s n c)").rearrange("(p f) -> p f", p=P)
    z_flat = z.rearrange("o (p t) k c -> p (o t k) c", t=T)
    mask_rows = mask.rearrange("o (p t) k -> p (o t) k", t=T)

    with ExitStack() as ctx:
        def sb(name, shape, dt):
            return ctx.enter_context(nc.sbuf_tensor(name, shape, dt))

        def sem(name):
            return ctx.enter_context(nc.semaphore(name))

        xa = sb("xa", [P, 2, R * T, C], F32)
        xs = sb("xs", [P, 2, R, T, 2 * C], F16)
        reg_a = sb("reg_a", [P, 4608], F32)
        reg_v = sb("reg_v", [P, 12288], F32)
        reg_g = sb("reg_g", [P, 9216], F32)
        reg_o = sb("reg_o", [P, 3072], F32)
        wth = sb("wth", [P, T, H, N], F16)
        reg_w = sb("reg_w", [P, 4608], F32)
        wtl = reg_w[:, :].bitcast(F16).rearrange("p (t h q) -> p t h q", t=T, h=H)
        xt = reg_a[:, 0:3072].bitcast(F16).rearrange("p (b q n) -> p b q n", b=2, q=PAIRS)
        sq = reg_a[:, 3072:4608].rearrange("p (r c) -> p r c", c=C)
        vh = reg_v[:, 0:6144].bitcast(F16).rearrange("p (b t h s c) -> p b t h s c", b=2, t=T, h=H, s=R)
        vl = reg_v[:, 6144:12288].bitcast(F16).rearrange("p (b t h s c) -> p b t h s c", b=2, t=T, h=H, s=R)
        gate = reg_g[:, 0:4096].rearrange("p (b s n) -> p b s n", b=2, s=R)
        gated = reg_g[:, 4096:8192].rearrange("p (b s n) -> p b s n", b=2, s=R)
        gth = reg_g[:, 8192:8704].bitcast(F16).rearrange("p (b n) -> p b n", b=2)
        gtl = reg_g[:, 8704:9216].bitcast(F16).rearrange("p (b n) -> p b n", b=2)
        ob = reg_o[:, :].rearrange("p (b s t c) -> p b s t c", b=2, s=R, t=T)
        xst = reg_a[:, 0:GRP * NX * 6].rearrange("p (g x s) -> p g x s", g=GRP, x=NX)
        xst3 = reg_a[:, 0:GRP * NX * 6].rearrange("p (g x s) -> p g x s", g=GRP, s=3)
        xch = reg_v[:, 0:2 * XB * C].rearrange("p (b n g e) -> p b n g e", b=2, n=XB, g=GRP)
        ztr = reg_v[:, 8192:12288].rearrange("p (b j n) -> p b j n", b=2, j=4)
        lg = reg_g[:, :].rearrange("p (t h k) -> p t h k", t=T, h=H)
        zst = reg_o[:, 0:2304].rearrange("p (k s) -> p k s", s=6)
        zq = reg_o[:, 2304:2304 + 2 * N].rearrange("p (a k) -> p a k", a=2)
        wvg = reg_w[0:C, 0:512]
        wvg_g = reg_w[0:C, 512:1024]
        bvg = reg_w[0:1, 1024:1536]
        wfull = reg_w[:, 1536:2048]
        centre_m = reg_w[:, 2048:2176]
        drop_m = reg_w[0:C, 2176:2304]
        beta_sel = reg_w[0:C, 2304:2432]
        bias_sel = reg_w[0:1, 2432:2560]
        ones_row = reg_w[0:1, 2560:2688]
        beta_zb = reg_w[:, 2688:2816]
        wo = reg_w[:, 3712:3840].rearrange("p (a n) -> p a n", a=2)
        wz = reg_w[:, 3840:3848]
        wz_g = reg_w[:, 3848:3856]
        zb = sb("zb", [P, 3, ZB, CZ], F32)
        lraw = sb("lraw", [P, 512], F32)
        mk = sb("mk", [P, N], F32)
        tmp = zb[:, 0, :, :].rearrange("p a b -> p (a b)")[:, 0:GRP * NX * 2].rearrange("p (g x) -> p g x", g=GRP)

        gn = zb[:, 1, :, :].rearrange("p a b -> p (a b)")[:, 0:6 * GRP].rearrange("p (a g) -> p a g", a=6)

        ident = sb("ident", [P, P], F32)
        ident16 = sb("ident16", [P, P], F16)
        mean_m = sb("mean_m", [P, P], F32)
        wvg_hi = sb("wvg_hi", [P, 2 * D], F16)
        wvg_lo = sb("wvg_lo", [P, 2 * D], F16)
        wo_hi = sb("wo_hi", [P, 2, C], F16)
        wo_lo = sb("wo_lo", [P, 2, C], F16)
        wzc = sb("wzc", [P, 32], F32)
        vec = sb("vec", [P, 4], F32)
        brow = sb("brow", [1, H + C], F32)
        bzo = sb("bzo", [P, H + C], F32)
        wmax = sb("wmax", [P, 3], F32)
        wmaxa = sb("wmaxa", [P, 3], F32)
        wpow = sb("wpow", [P, 3], F32)
        wscale = sb("wscale", [P, 3], F32)
        wback = sb("wback", [P, 3], F32)
        oscale = sb("oscale", [P, 1], F32)
        mhalf = sb("mhalf", [P, R * T], F32)
        eps_c = sb("eps_c", [P, 1], F32)
        gn_mean = sb("gn_mean", [P, C], F32)
        gn_rstd = sb("gn_rstd", [P, C], F32)
        ln_sum = sb("ln_sum", [P, R * T], F32)
        ln_mean = sb("ln_mean", [P, R * T], F32)
        ln_ssq = sb("ln_ssq", [P, R * T], F32)
        ln_var = sb("ln_var", [P, R * T], F32)
        ln_rstd = sb("ln_rstd", [P, R * T], F32)
        nmax = sb("nmax", [P, H], F32)
        esum = sb("esum", [P, H], F32)
        einv = sb("einv", [P, H], F32)

        bank = [ctx.enter_context(nc.psum_tensor(f"bank{i}", [P, 512], F32)) for i in range(8)]
        ps_o = bank[0:2]
        ps_xt = bank[2][:, 0:128].bitcast(F16)
        ps_gt, ps_v, ps_g, ps_p = bank[3], bank[4], bank[5], bank[6]
        ps_lg, ps_back, ps_w = bank[4], bank[5], bank[6:8]

        par_load = sem("par_load")
        mask_load = sem("mask_load")
        z_load = [sem(f"z_load{i}") for i in range(3)]
        xc_load = [sem(f"xc_load{i}") for i in range(2)]
        xa_load = [sem(f"xa_load{i}") for i in range(2)]
        res_load = [sem(f"res_load{i}") for i in range(2)]
        out_store = [sem(f"out_store{i}") for i in range(2)]
        consts = sem("consts")
        dlink = sem("dlink")
        prep_w = sem("prep_w")
        wprod = sem("wprod")
        wmax_ready = sem("wmax_ready")
        wmaxa_ready = sem("wmaxa_ready")
        w_ready = sem("w_ready")
        zt_pe = sem("zt_pe")
        zt_sb = sem("zt_sb")
        lg_pe = sem("lg_pe")
        lg_sb = sem("lg_sb")
        bk_pe = sem("bk_pe")
        bk_sb = sem("bk_sb")
        zst_done = sem("zst_done")
        xst_done = sem("xst_done")
        zvar_ready = sem("zvar_ready")
        zstd_ready = sem("zstd_ready")
        soft_in = sem("soft_in")
        soft_exp = sem("soft_exp")
        soft_w = sem("soft_w")
        wt_pe = sem("wt_pe")
        wh_sb = sem("wh_sb")
        wl_sb = sem("wl_sb")
        gn_part = sem("gn_part")
        gn_mm = sem("gn_mm")
        gn_var = sem("gn_var")
        gn_std = sem("gn_std")
        gn_ready = sem("gn_ready")
        ln_shifted = sem("ln_shifted")
        ln_scaled = sem("ln_scaled")
        ln_summed = sem("ln_summed")
        ln_mean_ok = sem("ln_mean_ok")
        ln_centred = sem("ln_centred")
        ln_squared = sem("ln_squared")
        ln_ssummed = sem("ln_ssummed")
        ln_var_ok = sem("ln_var_ok")
        ln_rstd_ok = sem("ln_rstd_ok")
        ln_normed = sem("ln_normed")
        xhi_done = sem("xhi_done")
        xlo_done = sem("xlo_done")
        xs_const = sem("xs_const")
        res_ready = sem("res_ready")
        xt_pe = sem("xt_pe")
        xt_sb = sem("xt_sb")
        v_pe = sem("v_pe")
        vh_sb = sem("vh_sb")
        vl_sb = sem("vl_sb")
        g_pe = sem("g_pe")
        g_sb = sem("g_sb")
        o_pe = sem("o_pe")
        gated_sb = sem("gated_sb")
        gt_pe = sem("gt_pe")
        gth_sb = sem("gth_sb")
        gtl_sb = sem("gtl_sb")
        p_pe = sem("p_pe")
        fin_sb = sem("fin_sb")

        block = ctx.enter_context(nc.Block())

        def passes(eng, t, body):
            if t == 0:
                body(0)
            with eng.Fori(1 if t == 0 else 0, QT_LOOPS) as i:
                body(i)

        def steps(eng, step):
            for c in range(-AHEAD, FIRST):
                step(0, c)
            with eng.Fori(0, LOOPS) as it:
                for c in range(FIRST, FIRST + PERIOD):
                    step(it, c)
            for c in range(FIRST, FIRST + STEPS + 5 - TAIL):
                step(LOOPS, c)

        def exists(it, c, shift):
            return not isinstance(it, int) or 0 <= PERIOD * it + c + shift < STEPS

        def wait(eng, s, it, per, n):
            if isinstance(it, int):
                if per * it + n > 0:
                    eng.wait_ge(s, per * it + n)
            else:
                assert per + n > 0
                eng.wait_ge(s, it * per + n)

        @block.sync
        def _(sp):
            sp.dma_start(wvg[:, 0:D], w_v).then_inc(par_load, 16)
            sp.dma_start(wvg[:, D:2 * D], w_g).then_inc(par_load, 16)
            sp.dma_start(bvg[:, 0:D], b_v.rearrange("(a n) -> a n", a=1)).then_inc(par_load, 16)
            sp.dma_start(bvg[:, D:2 * D], b_g.rearrange("(a n) -> a n", a=1)).then_inc(par_load, 16)
            sp.dma_start(wo[:, :, :], w_o.rearrange("(a p) n -> p a n", a=2)).then_inc(par_load, 16)
            sp.dma_start(wz[:, :], w_z).then_inc(par_load, 16)
            sp.dma_start(vec[:, 0:1], gamma_z.rearrange("(p a) -> p a", a=1)).then_inc(par_load, 16)
            sp.dma_start(vec[:, 1:2], beta_z.rearrange("(p a) -> p a", a=1)).then_inc(par_load, 16)
            sp.dma_start(vec[0:C, 2:3], gamma_m.rearrange("(p a) -> p a", a=1)).then_inc(par_load, 16)
            sp.dma_start(vec[0:C, 3:4], beta_m.rearrange("(p a) -> p a", a=1)).then_inc(par_load, 16)
            sp.dma_start(brow[:, 0:H], b_z.rearrange("(a n) -> a n", a=1)).then_inc(par_load, 16)
            sp.dma_start(brow[:, H:H + C], b_o.rearrange("(a n) -> a n", a=1)).then_inc(par_load, 16)
            def at(n, size):
                return n * size if isinstance(n, int) else sp.snap(n * size)

            def load_z(k, slot):
                sp.dma_start(zb[:, slot, :, :], z_flat[:, bass.ds(k, ZB), :]).then_inc(z_load[slot], 16)

            def load_chunk(f, slot):
                sp.dma_start(xch[:, slot, :, :, :].rearrange("p n g e -> p (n g e)"),
                             x_flat[:, bass.ds(f, XB * C)]).then_inc(xc_load[slot], 16)

            for n in range(3):
                load_z(n * ZB, n)
            for n in range(2):
                load_chunk(n * XB * C, n)
            with sp.Fori(0, T * QT_LOOPS - 1) as i:
                for b in range(ITER):
                    k = at(i * ITER + (b + 3), ZB)
                    turned, measured = at(i * ITER + (b + 1), 4), at(i * ITER + (b + 1), 1)
                    sp.wait_ge(zt_pe, turned)
                    sp.wait_ge(zst_done, measured)
                    load_z(k, b % 3)
                for e in range(2):
                    f = at(i * 2 + (e + 2), XB * C)
                    measured = at(i * 2 + (e + 1), 1)
                    sp.wait_ge(xst_done, measured)
                    load_chunk(f, e)
            for n in range(NB - 3, NB):
                sp.wait_ge(zt_pe, 4 * (n - 2))
                sp.wait_ge(zst_done, n - 2)
                load_z(n * ZB, n % 3)

            def load_x(row, slot):
                sp.dma_start(xa[:, slot, :, :].rearrange("p (s t) c -> p s (t c)", t=T),
                             x_rows[:, bass.ds(row, R), :]).then_inc(xa_load[slot], 16)

            def load_res(row, slot):
                sp.dma_start(ob[:, slot, :, :, :].rearrange("p s t c -> p s (t c)"),
                             x_rows[:, bass.ds(row, R), :]).then_inc(res_load[slot], 16)

            load_x(0, 0)
            load_x(R, 1)
            sp.wait_ge(soft_in, T)
            for m in range(2):
                load_res(m * R, m)
            for m in range(2, 4):
                sp.wait_ge(xhi_done, m - 1)
                sp.wait_ge(xlo_done, m - 1)
                load_x(m * R, m % 2)

            def serve(it, e, more_x, more_res):
                row, row_x, row_res = (at(it * 2 + (e + d), R) for d in (0, 4, 2))
                normed, ended, stored = at(it * 2 + (e + 3), 1), at(it * 2 + (e + 1), T), at(it + 1, 16)
                if more_x:
                    sp.wait_ge(xhi_done, normed)
                    sp.wait_ge(xlo_done, normed)
                    load_x(row_x, e)
                sp.wait_ge(fin_sb, ended)
                sp.dma_start(out_rows[:, bass.ds(row, R), :],
                             ob[:, e, :, :, :].rearrange("p s t c -> p s (t c)")).then_inc(out_store[e], 16)
                sp.wait_ge(out_store[e], stored)
                if more_res:
                    load_res(row_res, e)

            with sp.Fori(0, NG // 2 - 2) as it:
                for e in range(2):
                    serve(it, e, True, True)
            for it in (NG // 2 - 2, NG // 2 - 1):
                for e in range(2):
                    serve(it, e, False, it == NG // 2 - 2)

        @block.gpsimd
        def _(pool):
            pool.memset(ident[:, :], 0.0).then_inc(consts, 1)
            pool.memset(drop_m[:, :], 0.0).then_inc(consts, 1)
            pool.memset(beta_sel[:, :], 0.0).then_inc(consts, 1)
            pool.memset(bias_sel[:, :], 0.0).then_inc(consts, 1)
            pool.wait_ge(consts, 4)
            pool.affine_select(out=ident[:, :], in_=ident[:, :], compare_op=ALU.not_equal, fill=1.0, base=0,
                               pattern=[[-1, P]], channel_multiplier=1).then_inc(consts, 1)
            pool.affine_select(out=drop_m[:, :], in_=drop_m[:, :], compare_op=ALU.not_equal, fill=-1.0,
                               base=-(C - 1), pattern=[[0, P]], channel_multiplier=1).then_inc(consts, 1)
            pool.wait_ge(consts, 6)
            pool.affine_select(out=drop_m[:, :], in_=drop_m[:, :], compare_op=ALU.not_equal, fill=1.0, base=0,
                               pattern=[[0, 2], [-1, C]], channel_multiplier=1).then_inc(consts, 1)
            pool.wait_ge(consts, 7)
            for c in (C - 1, 2 * C - 1):
                pool.memset(drop_m[:, c:c + 1], 0.0).then_inc(consts, 1)
                pool.memset(bias_sel[:, c:c + 1], 1.0).then_inc(consts, 1)
            pool.memset(ones_row[:, :], 1.0).then_inc(consts, 1)
            pool.memset(mean_m[:, :], 1.0 / P).then_inc(consts, 1)
            pool.memset(wzc[:, :], 0.0).then_inc(consts, 1)
            pool.memset(eps_c[:, :], EPS).then_inc(consts, 1)
            pool.memset(mhalf[:, :], -0.5).then_inc(consts, 1)
            for b in range(2):
                pool.memset(xs[:, b, :, :, C - 1:C], 1.0).then_inc(xs_const, 1)
                pool.memset(xs[:, b, :, :, 2 * C - 1:2 * C], 0.0).then_inc(xs_const, 1)
            pool.wait_ge(wmax_ready, 1)
            pool.partition_all_reduce(wmaxa[:, :], wmax[:, :], P, ABSMAX).then_inc(wmaxa_ready, 1)

            for t in range(T):
                if t:
                    pool.wait_ge(soft_in, t)
                pool.dma_start(mk[:, :], mask_rows[:, t, :]).then_inc(mask_load, 16)

            pool.wait_ge(gn_ready, 2)
            mean_b = gn_mean[:, :].unsqueeze(1).broadcast_to([P, R * T, C])
            rstd_b = gn_rstd[:, :].unsqueeze(1).broadcast_to([P, R * T, C])
            bo_b = bzo[:, H:H + C].unsqueeze(1).broadcast_to([P, R * T, C])
            lnm_b = ln_mean[:, :].unsqueeze(2).broadcast_to([P, R * T, C])
            lnr_b = ln_rstd[:, :].unsqueeze(2).broadcast_to([P, R * T, C])

            def normalise(it, e):
                a = xa[:, e, :, :]
                wait(pool, xa_load[e], it, 16, 16)
                pool.tensor_tensor(a, a, mean_b, op=ALU.subtract).then_inc(ln_shifted, 1)
                wait(pool, ln_shifted, it, 2, e + 1)
                pool.tensor_tensor(a, a, rstd_b, op=ALU.mult).then_inc(ln_scaled, 1)
                wait(pool, ln_mean_ok, it, 2, e + 1)
                pool.tensor_tensor(a, a, lnm_b, op=ALU.subtract).then_inc(ln_centred, 1)
                wait(pool, ln_var_ok, it, 2, e + 1)
                pool.tensor_tensor(ln_rstd[:, :], ln_var[:, :], mhalf[:, :], op=ALU.pow).then_inc(ln_rstd_ok, 1)
                wait(pool, ln_rstd_ok, it, 2, e + 1)
                pool.tensor_tensor(a, a, lnr_b, op=ALU.mult).then_inc(ln_normed, 1)
                wait(pool, xhi_done, it, 2, e + 1)
                lo = xs[:, e, :, :, C:2 * C - 1].rearrange("p s t c -> p (s t) c")
                hi = xs[:, e, :, :, 0:C - 1].rearrange("p s t c -> p (s t) c")
                pool.tensor_tensor(lo, a[:, :, 0:C - 1], hi, op=ALU.subtract).then_inc(xlo_done, 1)

            def residual(it, e):
                r = ob[:, e, :, :, :].rearrange("p s t c -> p (s t) c")
                wait(pool, res_load[e], it, 16, 16)
                pool.tensor_tensor(r, r, bo_b, op=ALU.add).then_inc(res_ready, 1)

            normalise(0, 0)
            with pool.Fori(0, NG // 2 - 1) as it:
                normalise(it, 1)
                residual(it, 0)
                normalise(it + 1, 0)
                residual(it, 1)
            normalise(NG // 2 - 1, 1)
            residual(NG // 2 - 1, 0)
            residual(NG // 2 - 1, 1)

        @block.scalar
        def _(act):
            w_done = 0
            for t in range(T):
                def turn(i, t=t):
                    for b in range(ITER + 1):
                        n = t * QT_LOOPS * ITER + b
                        if b < ITER:
                            wait(act, lg_pe, i, ITER, n - 1)
                            for j in range(4):
                                wait(act, zt_pe, i, 4 * ITER, 4 * n + j + 1)
                                act.activation(ztr[:, b % 2, j, :], bank[j][:, :], ACT.Copy).then_inc(zt_sb, 1)
                        if b:
                            wait(act, lg_pe, i, ITER, n)
                            wait(act, bk_pe, i, ITER, n - 1)
                            act.activation(lraw[:, :], ps_lg[:, :], ACT.Copy).then_inc(lg_sb, 1)

                passes(act, t, turn)
                act.wait_ge(zvar_ready, t + 1)
                act.activation(zq[:, 1, :], zq[:, 0, :], ACT.Sqrt).then_inc(zstd_ready, 1)
                act.wait_ge(soft_in, t + 1)
                for h in range(H):
                    act.activation(lg[:, t, h, :], lg[:, t, h, :], ACT.Exp, bias=nmax[:, h:h + 1],
                                   accum_out=esum[:, h:h + 1]).then_inc(soft_exp, 1)
                for k in range(T):
                    for h in range(0, H, 4):
                        act.wait_ge(wt_pe, w_done + 1)
                        act.activation(wth[:, k, h:h + 4, t * P:(t + 1) * P],
                                       ps_w[w_done % 2][:, :].rearrange("p (h q) -> p h q", h=4), ACT.Copy)\
                           .then_inc(wh_sb, 1)
                        w_done += 1
            act.wait_ge(gn_var, 1)
            act.activation(gn[:, 5, :], gn[:, 4, :], ACT.Sqrt).then_inc(gn_std, 1)

            def step(it, c):
                two = lambda off: (off % PERIOD) // PAIRS
                if exists(it, c, -4):
                    q = c - 4
                    wait(act, gt_pe, it, PERIOD, q + 1)
                    wait(act, p_pe, it, PERIOD, q - 1)
                    act.activation(gth[:, q % 2, :], ps_gt[:, :], ACT.Copy).then_inc(gth_sb, 1)
                if exists(it, c, 12):
                    q = c + 12
                    t, sp_ = q % PAIRS // 4, q % 4
                    wait(act, v_pe, it, PERIOD, q + 1)
                    if q % PAIRS == 0:
                        wait(act, o_pe, it, PERIOD, q - PAIRS)
                    act.activation(vh[:, two(q), t, :, 2 * sp_:2 * sp_ + 2, :].rearrange("p h s c -> p s h c"),
                                   ps_v[:, :].rearrange("p (s h c) -> p s h c", s=2, h=H), ACT.Copy)\
                       .then_inc(vh_sb, 1)
                if exists(it, c, 4):
                    q = c + 4
                    wait(act, g_pe, it, PERIOD, q + 1)
                    if q % 4 == 0:
                        wait(act, gated_sb, it, PERIOD, q - 4)
                    act.activation(gate[:, q // 4 % 2, 2 * (q % 4):2 * (q % 4) + 2, :]
                                   .rearrange("p s n -> p (s n)"), ps_g[:, :], ACT.Sigmoid,
                                   scale=wback[:, 1:2]).then_inc(g_sb, 1)
                m, at = (c + 7) // PAIRS + 1, (c + 7) % PAIRS
                if at == 0 and exists(it, c, 19):
                    wait(act, ln_centred, it, 2, m + 1)
                    act.activation(sq, xa[:, m % 2, :, :], ACT.Square).then_inc(ln_squared, 1)
                m, at = (c + 3) // PAIRS + 1, (c + 3) % PAIRS
                if at == 0 and exists(it, c, 15):
                    wait(act, ln_normed, it, 2, m + 1)
                    wait(act, xt_pe, it, PERIOD, PAIRS * (m - 1))
                    act.activation(xs[:, m % 2, :, :, 0:C - 1].rearrange("p s t c -> p (s t) c"),
                                   xa[:, m % 2, :, 0:C - 1], ACT.Copy).then_inc(xhi_done, 1)

            steps(act, step)

        @block.vector
        def _(dve):
            links = [0]

            def link(ins):
                ins.then_inc(dlink, 1)
                links[0] += 1
                dve.wait_ge(dlink, links[0])

            dve.wait_ge(par_load, 12 * 16)
            dve.wait_ge(consts, 16)
            dve.tensor_copy(ident16[:, :], ident[:, :])
            dve.tensor_tensor(centre_m[:, :], ident[:, :], mean_m[:, :], op=ALU.subtract)
            dve.tensor_copy(beta_sel[:, C - 1:C], vec[0:C, 3:4])
            dve.tensor_copy(beta_sel[:, 2 * C - 1:2 * C], vec[0:C, 3:4])
            dve.tensor_scalar(wvg_g[:, :], wvg[:, :], vec[0:C, 2:3], None, ALU.mult)
            dve.tensor_scalar(wz_g[:, :], wz[:, :], vec[:, 0:1], None, ALU.mult)
            dve.tensor_scalar(beta_zb[:, :], mean_m[:, :], float(P), vec[:, 1:2], ALU.mult, ALU.mult)\
               .then_inc(prep_w, 1)
            dve.wait_ge(wprod, 1)
            dve.tensor_copy(wzc[:, 0:H], bank[7][:, 0:H])
            dve.tensor_copy(bzo[:, :], bank[7][:, H:2 * H + C])
            link(dve.tensor_copy(wfull[:, :], bank[6][:, :]))
            for i in range(2):
                dve.tensor_reduce(wmax[:, i:i + 1], wfull[:, i * D:(i + 1) * D], axis=AX_X, op=ALU.max,
                                  apply_absolute_value=True)
            dve.tensor_reduce(wmax[:, 2:3], wo[:, :, :].rearrange("p a n -> p (a n)"), axis=AX_X, op=ALU.max,
                              apply_absolute_value=True).then_inc(wmax_ready, 1)
            dve.wait_ge(wmaxa_ready, 1)
            link(dve.tensor_scalar(wmaxa[:, :], wmaxa[:, :], 1e-30, None, ALU.max))
            link(dve.tensor_scalar(wpow[:, :].bitcast(I32), wmaxa[:, :].bitcast(I32), 0x7F800000, None,
                                   ALU.bitwise_and))
            link(dve.reciprocal(wscale[:, :], wpow[:, :]))
            dve.tensor_scalar(wback[:, :], wpow[:, :], 1.0 / W_TARGET, None, ALU.mult)
            link(dve.tensor_scalar(wscale[:, :], wscale[:, :], W_TARGET, None, ALU.mult))
            dve.tensor_tensor(oscale[:, :], wback[:, 0:1], wback[:, 2:3], op=ALU.mult)
            for i in range(2):
                dve.tensor_scalar(wvg_hi[:, i * D:(i + 1) * D], wfull[:, i * D:(i + 1) * D], wscale[:, i:i + 1],
                                  None, ALU.mult)
            link(dve.tensor_scalar(wo_hi[:, :, :], wo[:, :, :], wscale[:, 2:3], None, ALU.mult))
            for i in range(2):
                dve.scalar_tensor_tensor(wvg_lo[:, i * D:(i + 1) * D], wfull[:, i * D:(i + 1) * D],
                                         wscale[:, i:i + 1], wvg_hi[:, i * D:(i + 1) * D], ALU.mult, ALU.subtract)
            dve.scalar_tensor_tensor(wo_lo[:, :, :], wo[:, :, :], wscale[:, 2:3], wo_hi[:, :, :],
                                     ALU.mult, ALU.subtract).then_inc(w_ready, 1)

            w_done = 0
            for t in range(T):
                def measure(i, t=t):
                    def keep_logits(b):
                        n = t * QT_LOOPS * ITER + b
                        wait(dve, bk_pe, i, ITER, n + 1)
                        dve.tensor_copy(
                            lg[:, t, :, bass.ds(i * (ITER * ZB) + b * ZB, ZB)]
                            .rearrange("p h (j k) -> p h j k", k=4),
                            ps_back[:, :].rearrange("p (k j h) -> p h j k", k=4, j=4)[:, 0:H, :, :])\
                           .then_inc(bk_sb, 1)

                    for b in range(ITER):
                        n = t * QT_LOOPS * ITER + b
                        wait(dve, z_load[b % 3], i, 32, 16 * (n // 3 + 1))
                        for k in range(ZB):
                            last = dve.bn_stats(zst[:, bass.ds(i * (ITER * ZB) + (b * ZB + k), 1), :]
                                                .rearrange("p k s -> p (k s)"), zb[:, b % 3, k, :])
                        last.then_inc(zst_done, 1)
                        if b >= 2:
                            keep_logits(b - 2)
                    for e in range(2):
                        m = t * QT_LOOPS * 2 + e
                        wait(dve, xc_load[e], i, 16, 16 * (m // 2 + 1))
                        for g in range(GRP):
                            last = dve.bn_stats(xst[:, g, bass.ds(i * 2 + m, 1), :]
                                                .rearrange("p x s -> p (x s)"), xch[:, e, :, g, :])
                        last.then_inc(xst_done, 1)
                        keep_logits(ITER - 2 + e)

                passes(dve, t, measure)
                dve.wait_ge(zst_done, (t + 1) * QT_LOOPS * ITER)
                dve.wait_ge(bk_sb, (t + 1) * QT_LOOPS * ITER)
                link(dve.tensor_tensor(zq[:, 0, :], zst[:, :, 1], zst[:, :, 4], op=ALU.subtract))
                link(dve.scalar_tensor_tensor(zq[:, 1, :], zq[:, 0, :], 0.25, zq[:, 0, :], ALU.mult, ALU.mult))
                link(dve.tensor_tensor(zq[:, 0, :], zst[:, :, 2], zst[:, :, 5], op=ALU.add))
                link(dve.scalar_tensor_tensor(zq[:, 0, :], zq[:, 0, :], 1.0 / CZ, zq[:, 1, :], ALU.mult, ALU.add))
                dve.tensor_scalar(zq[:, 0, :], zq[:, 0, :], EPS, None, ALU.add).then_inc(zvar_ready, 1)
                dve.wait_ge(mask_load, 16 * (t + 1))
                link(dve.tensor_scalar(mk[:, :], mk[:, :], -1.0, INF, ALU.add, ALU.mult))
                dve.wait_ge(zstd_ready, t + 1)
                link(dve.reciprocal(zq[:, 0, :], zq[:, 1, :]))
                link(dve.tensor_tensor(lg[:, t, :, :], lg[:, t, :, :],
                                       zq[:, 0, :].unsqueeze(1).broadcast_to([P, H, N]), op=ALU.mult))
                for h in range(H):
                    last = dve.scalar_tensor_tensor(lg[:, t, h, :], lg[:, t, h, :], bzo[:, h:h + 1], mk[:, :],
                                                    ALU.add, ALU.add)
                link(last)
                dve.tensor_reduce(nmax[:, :], lg[:, t, :, :], axis=AX_X, op=ALU.max, negate=True)\
                   .then_inc(soft_in, 1)
                dve.wait_ge(soft_exp, H * (t + 1))
                link(dve.reciprocal(einv[:, :], esum[:, :]))
                link(dve.tensor_scalar(einv[:, :], einv[:, :], W_SCALE, None, ALU.mult))
                dve.tensor_tensor(lg[:, t, :, :], lg[:, t, :, :],
                                  einv[:, :].unsqueeze(2).broadcast_to([P, H, N]), op=ALU.mult).then_inc(soft_w, 1)
                for k in range(T):
                    for h in range(0, H, 4):
                        dve.wait_ge(wh_sb, w_done + 1)
                        w_hi = wth[:, k, h:h + 4, t * P:(t + 1) * P]
                        w_lo = wtl[:, k, h:h + 4, t * P:(t + 1) * P]
                        dve.tensor_tensor(w_lo, ps_w[w_done % 2][:, :].rearrange("p (h q) -> p h q", h=4), w_hi,
                                          op=ALU.subtract).then_inc(wl_sb, 1)
                        w_done += 1

            cnt = 2 * NX
            dve.wait_ge(xst_done, NX)
            link(dve.tensor_reduce(gn[:, 0, :], xst3[:, :, :, 1], axis=AX_X, op=ALU.add))
            link(dve.tensor_scalar(gn[:, 0, :], gn[:, 0, :], 1.0 / cnt, None, ALU.mult))
            nop = dve.tensor_copy(gn[:, 1, :], gn[:, 0, :])
            nop.then_inc(gn_part, 1)
            link(dve.tensor_tensor(tmp, xst3[:, :, :, 1], gn[:, 0, :].unsqueeze(2).broadcast_to([P, GRP, cnt]),
                                   op=ALU.subtract))
            link(dve.tensor_tensor(tmp, tmp, tmp, op=ALU.mult))
            link(dve.tensor_reduce(gn[:, 2, :], tmp, axis=AX_X, op=ALU.add))
            link(dve.tensor_reduce(gn[:, 3, :], xst3[:, :, :, 2], axis=AX_X, op=ALU.add))
            link(dve.scalar_tensor_tensor(gn[:, 2, :], gn[:, 2, :], float(XB), gn[:, 3, :], ALU.mult, ALU.add))
            dve.wait_ge(gn_mm, 1)
            for e in range(2):
                dve.tensor_copy(gn_mean[:, :].rearrange("p (g e) -> p g e", e=2)[:, :, e], ps_w[1][:, 0:GRP])
            link(dve.tensor_tensor(gn[:, 3, :], gn[:, 0, :], ps_w[1][:, 0:GRP], op=ALU.subtract))
            link(dve.tensor_tensor(gn[:, 3, :], gn[:, 3, :], gn[:, 3, :], op=ALU.mult))
            dve.scalar_tensor_tensor(gn[:, 2, :], gn[:, 2, :], 1.0 / (cnt * XB), gn[:, 3, :],
                                     ALU.mult, ALU.add).then_inc(gn_part, 1)
            dve.wait_ge(gn_mm, 2)
            dve.tensor_scalar(gn[:, 4, :], ps_w[1][:, GRP:2 * GRP], EPS, None, ALU.add).then_inc(gn_var, 1)
            dve.wait_ge(gn_std, 1)
            link(dve.reciprocal(gn[:, 3, :], gn[:, 5, :]))
            for e in range(2):
                dve.tensor_copy(gn_rstd[:, :].rearrange("p (g e) -> p g e", e=2)[:, :, e], gn[:, 3, :])\
                   .then_inc(gn_ready, 1)

            def step(it, c):
                two = lambda off: (off % PERIOD) // PAIRS
                if exists(it, c, 13):
                    q = c + 13
                    wait(dve, xt_pe, it, PERIOD, q + 1)
                    if q % PAIRS == 0:
                        wait(dve, g_pe, it, PERIOD, q - PAIRS)
                    dve.tensor_copy(xt[:, two(q), q % PAIRS, :], ps_xt).then_inc(xt_sb, 1)
                if exists(it, c, -4):
                    q = c - 4
                    wait(dve, gth_sb, it, PERIOD, q + 1)
                    dve.tensor_tensor(gtl[:, q % 2, :], ps_gt[:, :], gth[:, q % 2, :], op=ALU.subtract)\
                       .then_inc(gtl_sb, 1)
                if exists(it, c, 0):
                    q, f, hp = c, c // 4, c % 4
                    wait(dve, o_pe, it, PERIOD, q + 1)
                    if hp == 0:
                        wait(dve, g_sb, it, PERIOD, q + 4)
                        wait(dve, gt_pe, it, PERIOD, q - 4)
                    heads = slice(2 * hp * (D // H), (2 * hp + 2) * (D // H))
                    dve.scalar_tensor_tensor(gated[:, f % 2, :, heads],
                                             ps_o[q % 2][:, :].rearrange("p (s n) -> p s n", s=R), 1.0 / W_SCALE,
                                             gate[:, f % 2, :, heads], ALU.mult, ALU.mult).then_inc(gated_sb, 1)
                if exists(it, c, 12):
                    q = c + 12
                    t, sp_ = q % PAIRS // 4, q % 4
                    wait(dve, vh_sb, it, PERIOD, q + 1)
                    view = lambda v: v[:, two(q), t, :, 2 * sp_:2 * sp_ + 2, :].rearrange("p h s c -> p s h c")
                    dve.tensor_tensor(view(vl), ps_v[:, :].rearrange("p (s h c) -> p s h c", s=2, h=H), view(vh),
                                      op=ALU.subtract).then_inc(vl_sb, 1)
                if c % 4 == 0 and exists(it, c, -8):
                    f = c // 4 - 2
                    t, n = f % T, f // T
                    wait(dve, p_pe, it, PERIOD, 4 * f + 4)
                    wait(dve, res_ready, it, 2, n + 1)
                    o = ob[:, n % 2, :, t, :]
                    dve.scalar_tensor_tensor(o, ps_p[:, :].rearrange("p (s c) -> p s c", s=R), oscale[:, 0:1], o,
                                             ALU.mult, ALU.add).then_inc(fin_sb, 1)
                m, at = (c + 9) // PAIRS + 1, (c + 9) % PAIRS
                if at == 0 and exists(it, c, 21):
                    wait(dve, ln_scaled, it, 2, m + 1)
                    dve.tensor_reduce(ln_sum[:, :], xa[:, m % 2, :, :], axis=AX_X, op=ALU.add).then_inc(ln_summed, 1)
                    wait(dve, ln_summed, it, 2, m + 1)
                    dve.tensor_scalar(ln_mean[:, :], ln_sum[:, :], 1.0 / C, None, ALU.mult).then_inc(ln_mean_ok, 1)
                m, at = (c + 6) // PAIRS + 1, (c + 6) % PAIRS
                if at == 0 and exists(it, c, 18):
                    wait(dve, ln_squared, it, 2, m + 1)
                    dve.tensor_reduce(ln_ssq[:, :], sq, axis=AX_X, op=ALU.add).then_inc(ln_ssummed, 1)
                    wait(dve, ln_ssummed, it, 2, m + 1)
                    dve.tensor_scalar(ln_var[:, :], ln_ssq[:, :], 1.0 / C, EPS, ALU.mult, ALU.add)\
                       .then_inc(ln_var_ok, 1)

            steps(dve, step)

        @block.tensor
        def _(pe):
            mm = nc.tensor.matmul
            pe.wait_ge(consts, 16)
            pe.wait_ge(prep_w, 1)
            mm(bank[6][:, :], drop_m[:, :], wvg_g[:, :], start=True, stop=False)
            mm(bank[6][:, :], beta_sel[:, :], wvg[:, :], start=False, stop=False)
            mm(bank[6][:, :], bias_sel[:, :], bvg[:, :], start=False, stop=True)
            mm(bank[7][:, 0:H], centre_m[:, :], wz_g[:, :], start=True, stop=True)
            mm(bank[7][:, H:2 * H], beta_zb[:, :], wz[:, :], start=True, stop=False)
            mm(bank[7][:, H:2 * H], ones_row[:, :], brow[:, 0:H], start=False, stop=True)
            mm(bank[7][:, 2 * H:2 * H + C], ones_row[:, :], brow[:, H:H + C], start=True, stop=True)\
                .then_inc(wprod, 1)
            pe.wait_ge(w_ready, 1)

            w_done = 0
            for t in range(T):
                def logits(i, t=t):
                    for b in range(ITER + 2):
                        n = t * QT_LOOPS * ITER + b
                        if b < ITER:
                            wait(pe, z_load[b % 3], i, 32, 16 * (n // 3 + 1))
                            for j in range(4):
                                wait(pe, zt_sb, i, 4 * ITER, 4 * n + j - 3)
                                for k in range(4):
                                    last = nc.tensor.transpose(bank[j][:, k * P:(k + 1) * P],
                                                               zb[:, b % 3, 4 * j + k, :], ident[:, :])
                                last.then_inc(zt_pe, 1)
                        if b >= 2:
                            wait(pe, lg_sb, i, ITER, n - 1)
                            wait(pe, bk_sb, i, ITER, n - 2)
                            for k in range(4):
                                last = nc.tensor.transpose(ps_back[:, k * P:(k + 1) * P],
                                                           lraw[:, k * P:(k + 1) * P], ident[:, :])
                            last.then_inc(bk_pe, 1)
                        if 1 <= b <= ITER:
                            wait(pe, zt_sb, i, 4 * ITER, 4 * n)
                            wait(pe, lg_sb, i, ITER, n - 1)
                            for j in range(4):
                                last = mm(ps_lg[32 * j:32 * j + 32, :], wzc[:, :], ztr[:, (b - 1) % 2, j, :],
                                          start=True, stop=True)
                            last.then_inc(lg_pe, 1)

                passes(pe, t, logits)
                pe.wait_ge(soft_w, t + 1)
                for k in range(T):
                    for h in range(0, H, 4):
                        if w_done >= 2:
                            pe.wait_ge(wl_sb, w_done - 1)
                        for j in range(4):
                            blk = lg[:, t, h + j, :].rearrange("p (k t) -> p t k", t=T)[:, k, :]
                            last = nc.tensor.transpose(ps_w[w_done % 2][:, j * P:(j + 1) * P], blk, ident[:, :])
                        last.then_inc(wt_pe, 1)
                        w_done += 1
            pe.wait_ge(wl_sb, w_done)
            for i, src in enumerate((1, 2)):
                pe.wait_ge(gn_part, i + 1)
                mm(ps_w[1][:, i * GRP:(i + 1) * GRP], mean_m[:, :], gn[:, src, :], start=True, stop=True)\
                    .then_inc(gn_mm, 1)

            pe.wait_ge(bk_sb, NB)
            pe.wait_ge(xs_const, 4)

            def step(it, c):
                two = lambda off: (off % PERIOD) // PAIRS

                def average(hh):
                    q, t, h = c, c % PAIRS // 4, 2 * (c % 4) + hh
                    for k in range(T):
                        w_hi, w_lo = wth[:, k, h, t * P:(t + 1) * P], wtl[:, k, h, t * P:(t + 1) * P]
                        v_hi, v_lo = vh[:, two(q), k, h, :, :], vl[:, two(q), k, h, :, :]
                        o = ps_o[q % 2][:, :].rearrange("p (s h c) -> p h s c", s=R, h=2)[:, hh, :, :]
                        mm(o, w_hi, v_hi, start=k == 0, stop=False)
                        mm(o, w_hi, v_lo, start=False, stop=False)
                        last = mm(o, w_lo, v_hi, start=False, stop=k == T - 1)
                    if hh == 1:
                        last.then_inc(o_pe, 1)

                if exists(it, c, 0):
                    wait(pe, gated_sb, it, PERIOD, c - 1)
                    if c % PAIRS == 0:
                        wait(pe, vh_sb, it, PERIOD, c + PAIRS)
                        wait(pe, vl_sb, it, PERIOD, c + PAIRS)
                    average(0)
                if exists(it, c, 13):
                    q = c + 13
                    t, sp_ = q % PAIRS // 4, q % 4
                    if q % PAIRS == 0:
                        wait(pe, xhi_done, it, 2, q // PAIRS + 1)
                        wait(pe, xlo_done, it, 2, q // PAIRS + 1)
                    wait(pe, xt_sb, it, PERIOD, q)
                    for s in range(2):
                        last = nc.tensor.transpose(ps_xt[:, s * P:(s + 1) * P], xs[:, two(q), 2 * sp_ + s, t, :],
                                                   ident16[:, :])
                    last.then_inc(xt_pe, 1)
                if exists(it, c, -4):
                    q = c - 4
                    if q % 4 == 0:
                        wait(pe, gated_sb, it, PERIOD, q + 4)
                    wait(pe, gtl_sb, it, PERIOD, q)
                    for s in range(2):
                        for a in range(2):
                            blk = gated[:, q // 4 % 2, 2 * (q % 4) + s, a * P:(a + 1) * P]
                            last = nc.tensor.transpose(ps_gt[:, (2 * s + a) * P:(2 * s + a + 1) * P], blk,
                                                       ident[:, :])
                    last.then_inc(gt_pe, 1)
                if exists(it, c, 0):
                    average(1)
                for shift, ps, done, free, off in ((12, ps_v, v_pe, vl_sb, 0), (4, ps_g, g_pe, g_sb, D)):
                    if exists(it, c, shift):
                        q = c + shift
                        wait(pe, xt_sb, it, PERIOD, q + 1)
                        wait(pe, free, it, PERIOD, q)
                        for s in range(2):
                            x_t = xt[:, two(q), q % PAIRS, s * P:(s + 1) * P]
                            mm(ps[:, s * D:(s + 1) * D], x_t, wvg_hi[:, off:off + D], start=True, stop=False)
                            last = mm(ps[:, s * D:(s + 1) * D], x_t, wvg_lo[:, off:off + D], start=False, stop=True)
                        last.then_inc(done, 1)
                if exists(it, c, -5):
                    q = c - 5
                    wait(pe, gtl_sb, it, PERIOD, q + 1)
                    if q % 4 == 0:
                        wait(pe, fin_sb, it, 2 * T, q // 4)
                    for s in range(2):
                        o = ps_p[:, (2 * (q % 4) + s) * C:(2 * (q % 4) + s + 1) * C]
                        for a in range(2):
                            g_hi = gth[:, q % 2, (2 * s + a) * P:(2 * s + a + 1) * P]
                            g_lo = gtl[:, q % 2, (2 * s + a) * P:(2 * s + a + 1) * P]
                            mm(o, g_hi, wo_hi[:, a, :], start=a == 0, stop=False)
                            mm(o, g_hi, wo_lo[:, a, :], start=False, stop=False)
                            last = mm(o, g_lo, wo_hi[:, a, :], start=False, stop=a == 1)
                    last.then_inc(p_pe, 1)

            steps(pe, step)


_INS = ["x"] + ["L0_conv_" + n for n in ("z", "mask", "gamma_m", "beta_m", "gamma_z", "beta_z", "w_z", "b_z",
                                         "w_v", "b_v", "w_g", "b_g", "w_o", "b_o")]


def kernel(**inputs):
    import numpy as np
    import concourse.bacc as bacc
    from concourse.bass_utils import run_bass_kernel_spmd

    nc = bacc.Bacc("TRN2", target_bir_lowering=False, num_devices=1)
    arrays, args = {}, []
    for name in _INS:
        a = np.ascontiguousarray(inputs[name])
        arrays[f"in_{name}"] = a
        args.append(nc.dram_tensor(f"in_{name}", a.shape, mybir.dt.from_np(a.dtype), kind="ExternalInput").ap())
    args.append(nc.dram_tensor("out", arrays["in_x"].shape, F32, kind="ExternalOutput").ap())
    pair_weighted(nc, *args)
    return run_bass_kernel_spmd(nc, [arrays], core_ids=[0]).results[0]["out"]
```

```python
from contextlib import ExitStack

import concourse.bass as bass
from concourse import mybir

F32 = mybir.dt.float32
F16 = mybir.dt.float16
I32 = mybir.dt.int32
ALU = mybir.AluOpType
ACT = mybir.ActivationFunctionType
AX_X = mybir.AxisListType.X
ABSMAX = bass.bass_isa.ReduceOp.absmax

P = 128
EPS = 1e-5
INF = 1e9
W_SCALE = 2.0 ** 14
W_TARGET = 2.0 ** 7

R = 8
PAIRS = 12
PERIOD = 2 * PAIRS
FIRST = 24
AHEAD = 12
AFTER = 10


def pair_weighted(nc, x, z, mask, gamma_m, beta_m, gamma_z, beta_z, w_z, b_z, w_v, b_v, w_g, b_g, w_o, b_o, out):
    _, S, N, C = x.shape
    CZ = z.shape[-1]
    H = w_z.shape[-1]
    D = w_v.shape[-1]
    HC = D // H
    T = N // P
    NG = S // R
    STEPS = NG * PAIRS
    LOOPS = (STEPS - 41 - FIRST) // PERIOD
    TAIL = FIRST + LOOPS * PERIOD
    assert (T, C, CZ, H, D) == (3, 64, 128, 8, 256)

    ZB = 16
    ITER = 6
    QT_LOOPS = N // (ZB * ITER)
    NB = T * QT_LOOPS * ITER
    XB = 128
    NX = S * N // P // XB
    GRP = 32
    assert NX == T * QT_LOOPS

    x_rows = x.rearrange("o s (p t) c -> p (o s) (t c)", t=T)
    out_rows = out.rearrange("o s (p t) c -> p (o s) (t c)", t=T)
    x_flat = x.rearrange("o s n c -> (o s n c)").rearrange("(p f) -> p f", p=P)
    z_flat = z.rearrange("o (p t) k c -> p (o t k) c", t=T)
    mask_rows = mask.rearrange("o (p t) k -> p (o t) k", t=T)

    with ExitStack() as ctx:
        def sb(name, shape, dt):
            return ctx.enter_context(nc.sbuf_tensor(name, shape, dt))

        def sem(name):
            return ctx.enter_context(nc.semaphore(name))

        reg_x = sb("reg_x", [P, 6144], F32)
        reg_a = sb("reg_a", [P, 4608], F32)
        reg_v = sb("reg_v", [P, 12288], F32)
        reg_g = sb("reg_g", [P, 9216], F32)
        reg_o = sb("reg_o", [P, 3072], F32)
        reg_z = sb("reg_z", [P, 6144], F32)
        wth = sb("wth", [P, T, H, N], F16)
        reg_w = sb("reg_w", [P, 4608], F32)
        wtl = reg_w[:, :].bitcast(F16).rearrange("p (t h q) -> p t h q", t=T, h=H)
        xa = reg_x[:, 0:3072].rearrange("p (b r c) -> p b r c", b=2, c=C)
        xs = reg_x[:, 3072:6144].bitcast(F16).rearrange("p (b t s c) -> p b t s c", b=2, s=R, t=T)
        xt = reg_a[:, 0:3072].bitcast(F16).rearrange("p (b t s n) -> p b t s n", b=2, t=T, s=R)
        sq = reg_a[:, 3072:4608].rearrange("p (r c) -> p r c", c=C)
        vh = reg_v[:, 0:6144].bitcast(F16).rearrange("p (b t h s c) -> p b t h s c", b=2, t=T, h=H, s=R)
        vl = reg_v[:, 6144:12288].bitcast(F16).rearrange("p (b t h s c) -> p b t h s c", b=2, t=T, h=H, s=R)
        gate = reg_g[:, 0:4096].rearrange("p (b s n) -> p b s n", b=2, s=R)
        gated = reg_g[:, 4096:5120].rearrange("p (b s n) -> p b s n", b=2, s=R)
        gh = reg_g[:, 5120:9216].bitcast(F16).rearrange("p (b a l s n) -> p b a l s n", b=2, a=2, l=2, s=R)
        gt = reg_z[:, :].bitcast(F16).rearrange("p (b a l s n) -> p b a l s n", b=3, a=2, l=2, s=R)
        ob = reg_o[:, :].rearrange("p (b s t c) -> p b s t c", b=2, s=R, t=T)
        xst = reg_a[:, 0:GRP * NX * 6].rearrange("p (g x s) -> p g x s", g=GRP, x=NX)
        xst3 = reg_a[:, 0:GRP * NX * 6].rearrange("p (g x s) -> p g x s", g=GRP, s=3)
        xch = reg_v[:, 0:XB * C].rearrange("p (n g e) -> p n g e", n=XB, g=GRP)
        ztr = reg_v[:, 8192:12288].rearrange("p (b j n) -> p b j n", b=2, j=4)
        lg = reg_g[:, :].rearrange("p (t h k) -> p t h k", t=T, h=H)
        zst = reg_o[:, 0:3 * N].rearrange("p (k s) -> p k s", s=3)
        zq = reg_o[:, 2304:2304 + 2 * N].rearrange("p (a k) -> p a k", a=2)
        wvg = reg_w[0:C, 0:512]
        wvg_g = reg_w[0:C, 512:1024]
        bvg = reg_w[0:1, 1024:1536]
        wfull = reg_w[:, 1536:2048]
        centre_m = reg_w[:, 2048:2176]
        drop_m = reg_w[0:C, 2176:2304]
        beta_sel = reg_w[0:C, 2304:2432]
        bias_sel = reg_w[0:1, 2432:2560]
        ones_row = reg_w[0:1, 2560:2688]
        beta_zb = reg_w[:, 2688:2816]
        wo = reg_w[:, 3712:3840].rearrange("p (a n) -> p a n", a=2)
        wz = reg_w[:, 3840:3848]
        wz_g = reg_w[:, 3848:3856]
        z_buf = [reg[:, i * ZB * CZ:(i + 1) * ZB * CZ].rearrange("p (k c) -> p k c", c=CZ)
                 for reg in (reg_z, reg_x) for i in range(3)]
        lraw = sb("lraw", [P, 512], F32)
        mk = sb("mk", [P, N], F32)
        tmp = reg_z[:, 0:GRP * NX * 2].rearrange("p (g x) -> p g x", g=GRP)

        gn = reg_z[:, 2048:2048 + 6 * GRP].rearrange("p (a g) -> p a g", a=6)

        ident = sb("ident", [P, P], F32)
        mean_m = sb("mean_m", [P, P], F32)
        wvg_hi = sb("wvg_hi", [P, 2 * D], F16)
        wvg_lo = sb("wvg_lo", [P, 2 * D], F16)
        wo_hi = sb("wo_hi", [P, 2, C], F16)
        wo_lo = sb("wo_lo", [P, 2, C], F16)
        wzc = sb("wzc", [P, 32], F32)
        vec = sb("vec", [P, 4], F32)
        brow = sb("brow", [1, H + C], F32)
        bzo = sb("bzo", [P, H + C], F32)
        wmax = sb("wmax", [P, 3], F32)
        wmaxa = sb("wmaxa", [P, 3], F32)
        wpow = sb("wpow", [P, 3], F32)
        wscale = sb("wscale", [P, 3], F32)
        wback = sb("wback", [P, 3], F32)
        oscale = sb("oscale", [P, 1], F32)
        mhalf = sb("mhalf", [P, R * T], F32)
        eps_c = sb("eps_c", [P, 1], F32)
        gn_mean = sb("gn_mean", [P, C], F32)
        gn_rstd = sb("gn_rstd", [P, C], F32)
        ln_sum = sb("ln_sum", [P, R * T], F32)
        ln_mean = sb("ln_mean", [P, R * T], F32)
        ln_ssq = sb("ln_ssq", [P, R * T], F32)
        ln_var = sb("ln_var", [P, R * T], F32)
        ln_rstd = sb("ln_rstd", [P, R * T], F32)
        nmax = sb("nmax", [P, H], F32)
        esum = sb("esum", [P, H], F32)
        einv = sb("einv", [P, H], F32)

        bank = [ctx.enter_context(nc.psum_tensor(f"bank{i}", [P, 512], F32)) for i in range(8)]
        ps_o = bank[0:2]
        ps_v, ps_g, ps_p = bank[2:4], bank[5], bank[6:8]
        ps_lg, ps_back, ps_w = bank[4], bank[5], bank[6:8]

        par_load = sem("par_load")
        mask_load = sem("mask_load")
        z_load = [sem(f"z_load{i}") for i in range(6)]
        xc_load = sem("xc_load")
        xa_load = [sem(f"xa_load{i}") for i in range(2)]
        res_load = [sem(f"res_load{i}") for i in range(2)]
        out_store = [sem(f"out_store{i}") for i in range(2)]
        consts = sem("consts")
        dlink = sem("dlink")
        prep_w = sem("prep_w")
        wprod = sem("wprod")
        wmax_ready = sem("wmax_ready")
        wmaxa_ready = sem("wmaxa_ready")
        w_ready = sem("w_ready")
        zt_pe = sem("zt_pe")
        zt_sb = sem("zt_sb")
        lg_pe = sem("lg_pe")
        lg_sb = sem("lg_sb")
        bk_pe = sem("bk_pe")
        bk_sb = sem("bk_sb")
        zst_done = sem("zst_done")
        xst_done = sem("xst_done")
        zvar_ready = sem("zvar_ready")
        zstd_ready = sem("zstd_ready")
        zinv_ready = sem("zinv_ready")
        lg_scaled = sem("lg_scaled")
        soft_in = sem("soft_in")
        esum_inv = sem("esum_inv")
        soft_exp = sem("soft_exp")
        soft_w = sem("soft_w")
        wt_pe = sem("wt_pe")
        wh_sb = sem("wh_sb")
        wl_sb = sem("wl_sb")
        gn_part = sem("gn_part")
        gn_mm = sem("gn_mm")
        gn_var = sem("gn_var")
        gn_std = sem("gn_std")
        gn_ready = sem("gn_ready")
        ln_shifted = sem("ln_shifted")
        ln_scaled = sem("ln_scaled")
        ln_summed = sem("ln_summed")
        ln_mean_ok = sem("ln_mean_ok")
        ln_centred = sem("ln_centred")
        ln_squared = sem("ln_squared")
        ln_ssummed = sem("ln_ssummed")
        ln_var_ok = sem("ln_var_ok")
        ln_rstd_ok = sem("ln_rstd_ok")
        ln_normed = sem("ln_normed")
        xhi_done = sem("xhi_done")
        xlo_done = sem("xlo_done")
        xs_const = sem("xs_const")
        res_ready = sem("res_ready")
        xt_turn = [[sem(f"xt_turn{b}{t}") for t in range(T)] for b in range(2)]
        v_pe = sem("v_pe")
        vh_sb = sem("vh_sb")
        vl_sb = sem("vl_sb")
        g_pe = sem("g_pe")
        g_sb = sem("g_sb")
        o_pe = sem("o_pe")
        gated_sb = sem("gated_sb")
        ghi_sb = sem("ghi_sb")
        glo_sb = sem("glo_sb")
        turn_next = sem("turn_next")
        gt_turn = [[sem(f"gt_turn{b}{a}") for a in range(2)] for b in range(2)]
        p_pe = sem("p_pe")
        fin_sb = sem("fin_sb")

        block = ctx.enter_context(nc.Block())

        loop_start = [0]

        def passes(eng, body):
            body(0, True)
            loop_start[0] = 1
            with eng.Fori(1, QT_LOOPS) as i:
                body(i, False)
            loop_start[0] = 0

        def steps(eng, step):
            for c in range(-AHEAD, FIRST):
                step(0, c)
            with eng.Fori(0, LOOPS) as it:
                for c in range(FIRST, FIRST + PERIOD):
                    step(it, c)
            for c in range(FIRST, FIRST + STEPS + AFTER - TAIL):
                step(LOOPS, c)

        def exists(it, c, shift):
            return not isinstance(it, int) or 0 <= PERIOD * it + c + shift < STEPS

        def wait(eng, s, it, per, n):
            if isinstance(it, int):
                if per * it + n > 0:
                    eng.wait_ge(s, per * it + n)
            else:
                assert per * loop_start[0] + n > 0
                eng.wait_ge(s, it * per + n)

        def divide_std(eng, t, half):
            hs = slice(4 * half, 4 * half + 4)
            return eng.tensor_tensor(lg[:, t, hs, :], lg[:, t, hs, :],
                                     zq[:, 0, :].unsqueeze(1).broadcast_to([P, 4, N]), op=ALU.mult)

        def divide_sum(eng, t, half):
            hs = slice(4 * half, 4 * half + 4)
            return eng.tensor_tensor(lg[:, t, hs, :], lg[:, t, hs, :],
                                     einv[:, hs].unsqueeze(2).broadcast_to([P, 4, N]), op=ALU.mult)

        @block.sync
        def _(sp):
            sp.dma_start(wvg[:, 0:D], w_v).then_inc(par_load, 16)
            sp.dma_start(wvg[:, D:2 * D], w_g).then_inc(par_load, 16)
            sp.dma_start(bvg[:, 0:D], b_v.rearrange("(a n) -> a n", a=1)).then_inc(par_load, 16)
            sp.dma_start(bvg[:, D:2 * D], b_g.rearrange("(a n) -> a n", a=1)).then_inc(par_load, 16)
            sp.dma_start(wo[:, :, :], w_o.rearrange("(a p) n -> p a n", a=2)).then_inc(par_load, 16)
            sp.dma_start(wz[:, :], w_z).then_inc(par_load, 16)
            sp.dma_start(vec[:, 0:1], gamma_z.rearrange("(p a) -> p a", a=1)).then_inc(par_load, 16)
            sp.dma_start(vec[:, 1:2], beta_z.rearrange("(p a) -> p a", a=1)).then_inc(par_load, 16)
            sp.dma_start(vec[0:C, 2:3], gamma_m.rearrange("(p a) -> p a", a=1)).then_inc(par_load, 16)
            sp.dma_start(vec[0:C, 3:4], beta_m.rearrange("(p a) -> p a", a=1)).then_inc(par_load, 16)
            sp.dma_start(brow[:, 0:H], b_z.rearrange("(a n) -> a n", a=1)).then_inc(par_load, 16)
            sp.dma_start(brow[:, H:H + C], b_o.rearrange("(a n) -> a n", a=1)).then_inc(par_load, 16)
            def at(n, size):
                return n * size if isinstance(n, int) else sp.snap(n * size)

            def load_z(k, slot):
                sp.dma_start(z_buf[slot], z_flat[:, bass.ds(k, ZB), :]).then_inc(z_load[slot], 16)

            def feed(i, more):
                f = at(i, XB * C)
                if not (isinstance(i, int) and i == 0):
                    taken = at(i, 1)
                    sp.wait_ge(xst_done, taken)
                sp.dma_start(xch.rearrange("p n g e -> p (n g e)"), x_flat[:, bass.ds(f, XB * C)])\
                  .then_inc(xc_load, 16)
                for b in range(ITER if more else 0):
                    k = at((i + 1) * ITER + b, ZB)
                    turned, measured = at(i * ITER + (b + 1), 4), at(i * ITER + (b + 1), 1)
                    sp.wait_ge(zt_pe, turned)
                    sp.wait_ge(zst_done, measured)
                    load_z(k, b)

            for n in range(ITER):
                load_z(n * ZB, n)
            feed(0, True)
            with sp.Fori(1, T * QT_LOOPS - 1) as i:
                feed(i, True)
            feed(T * QT_LOOPS - 1, False)

            def load_x(row, slot):
                sp.dma_start(xa[:, slot, :, :].rearrange("p (s t) c -> p s (t c)", t=T),
                             x_rows[:, bass.ds(row, R), :]).then_inc(xa_load[slot], 16)

            def load_res(row, slot):
                sp.dma_start(ob[:, slot, :, :, :].rearrange("p s t c -> p s (t c)"),
                             x_rows[:, bass.ds(row, R), :]).then_inc(res_load[slot], 16)

            sp.wait_ge(zt_pe, 4 * NB)
            sp.wait_ge(zst_done, NB)
            load_x(0, 0)
            load_x(R, 1)
            sp.wait_ge(soft_in, 2 * T)
            for m in range(2):
                load_res(m * R, m)

            def turn_x(t, b):
                sp.dma_start_transpose(xt[:, b, t, :, :], xs[:, b, t, :, :].rearrange("p s c -> p (s c)"))\
                  .then_inc(xt_turn[b][t], 16)

            sp.wait_ge(xs_const, 4)
            for m in range(2):
                if m == 0:
                    sp.wait_ge(xhi_done, 1)
                    sp.wait_ge(xlo_done, 1)
                    for t in range(T):
                        turn_x(t, 0)
                    load_x(2 * R, 0)

            def count(it, per, n):
                return per * it + n if isinstance(it, int) else sp.snap(it * per + n)

            def step(it, c):
                if c % 2 == 0 and exists(it, c, -1):
                    q = c - 1
                    f, a = q // 4, q % 4 // 2
                    wait(sp, glo_sb, it, PERIOD, q + 1)
                    sp.sem_inc(turn_next, 1)
                    sp.dma_start_transpose(
                        gt[:, f % 3, a, :, :, :].rearrange("p l s n -> p (l s) n"),
                        gh[:, f % 2, a, :, :, :].rearrange("p l s n -> p (l s n)")).then_inc(gt_turn[f % 2][a], 16)
                if c % 12 == 8 and exists(it, c, 16):
                    m = (c + 4) // PAIRS + 1
                    wait(sp, xlo_done, it, 2, m + 1)
                    sp.sem_inc(turn_next, 1)
                    for t in range(T):
                        turn_x(t, m % 2)
                    if exists(it, c, 16 + PERIOD):
                        load_x(count(it, 2 * R, (m + 2) * R), m % 2)
                if c % 12 == 9 and exists(it, c, -21):
                    n = (c - 21) // PAIRS
                    row, ended = count(it, 2 * R, n * R), count(it, 2 * T, T * (n + 1))
                    sp.wait_ge(fin_sb, ended)
                    sp.dma_start(out_rows[:, bass.ds(row, R), :],
                                 ob[:, n % 2, :, :, :].rearrange("p s t c -> p s (t c)"))\
                      .then_inc(out_store[n % 2], 16)
                if c % 12 == 11 and exists(it, c, 1) and exists(it, c, -23):
                    n = (c - 23) // PAIRS
                    row, stored = count(it, 2 * R, (n + 2) * R), count(it, 16, 16 * (n // 2 + 1))
                    sp.wait_ge(out_store[n % 2], stored)
                    load_res(row, n % 2)

            steps(sp, step)
            for b in range(2):
                sp.wait_ge(out_store[b], 16 * NG // 2)

        @block.gpsimd
        def _(pool):
            pool.memset(ident[:, :], 0.0).then_inc(consts, 1)
            pool.memset(drop_m[:, :], 0.0).then_inc(consts, 1)
            pool.memset(beta_sel[:, :], 0.0).then_inc(consts, 1)
            pool.memset(bias_sel[:, :], 0.0).then_inc(consts, 1)
            pool.wait_ge(consts, 4)
            pool.affine_select(out=ident[:, :], in_=ident[:, :], compare_op=ALU.not_equal, fill=1.0, base=0,
                               pattern=[[-1, P]], channel_multiplier=1).then_inc(consts, 1)
            pool.affine_select(out=drop_m[:, :], in_=drop_m[:, :], compare_op=ALU.not_equal, fill=-1.0,
                               base=-(C - 1), pattern=[[0, P]], channel_multiplier=1).then_inc(consts, 1)
            pool.wait_ge(consts, 6)
            pool.affine_select(out=drop_m[:, :], in_=drop_m[:, :], compare_op=ALU.not_equal, fill=1.0, base=0,
                               pattern=[[0, 2], [-1, C]], channel_multiplier=1).then_inc(consts, 1)
            pool.wait_ge(consts, 7)
            for c in (C - 1, 2 * C - 1):
                pool.memset(drop_m[:, c:c + 1], 0.0).then_inc(consts, 1)
                pool.memset(bias_sel[:, c:c + 1], 1.0).then_inc(consts, 1)
            pool.memset(ones_row[:, :], 1.0).then_inc(consts, 1)
            pool.memset(mean_m[:, :], 1.0 / P).then_inc(consts, 1)
            pool.memset(wzc[:, :], 0.0).then_inc(consts, 1)
            pool.memset(eps_c[:, :], EPS).then_inc(consts, 1)
            pool.memset(mhalf[:, :], -0.5).then_inc(consts, 1)
            pool.wait_ge(wmax_ready, 1)
            pool.partition_all_reduce(wmaxa[:, :], wmax[:, :], P, ABSMAX).then_inc(wmaxa_ready, 1)

            pool.dma_start(mk[:, :], mask_rows[:, 0, :]).then_inc(mask_load, 16)
            for t in range(T - 1):
                pool.wait_ge(bk_sb, (t + 1) * QT_LOOPS * ITER)
                pool.wait_ge(zinv_ready, t + 1)
                for half in range(2):
                    divide_std(pool, t, half).then_inc(lg_scaled, 1)
                pool.wait_ge(soft_in, 2 * (t + 1))
                pool.dma_start(mk[:, :], mask_rows[:, t + 1, :]).then_inc(mask_load, 16)
                for half in range(2):
                    pool.wait_ge(esum_inv, 2 * t + half + 1)
                    divide_sum(pool, t, half).then_inc(soft_w, 1)

            pool.wait_ge(zt_pe, 4 * NB)
            pool.wait_ge(zst_done, NB)
            for b in range(2):
                pool.memset(xs[:, b, :, :, C - 1:C], 1.0).then_inc(xs_const, 1)
                pool.memset(xs[:, b, :, :, 2 * C - 1:2 * C], 0.0).then_inc(xs_const, 1)
            pool.wait_ge(gn_ready, 2)
            mean_b = gn_mean[:, :].unsqueeze(1).broadcast_to([P, R * T, C])
            rstd_b = gn_rstd[:, :].unsqueeze(1).broadcast_to([P, R * T, C])
            bo_b = bzo[:, H:H + C].unsqueeze(1).broadcast_to([P, R * T, C])
            lnm_b = ln_mean[:, :].unsqueeze(2).broadcast_to([P, R * T, C])
            lnr_b = ln_rstd[:, :].unsqueeze(2).broadcast_to([P, R * T, C])

            def normalise(it, e):
                a = xa[:, e, :, :]
                wait(pool, xa_load[e], it, 16, 16)
                pool.tensor_tensor(a, a, mean_b, op=ALU.subtract).then_inc(ln_shifted, 1)
                wait(pool, ln_shifted, it, 2, e + 1)
                pool.tensor_tensor(a, a, rstd_b, op=ALU.mult).then_inc(ln_scaled, 1)
                wait(pool, ln_mean_ok, it, 2, e + 1)
                pool.tensor_tensor(a, a, lnm_b, op=ALU.subtract).then_inc(ln_centred, 1)
                wait(pool, ln_var_ok, it, 2, e + 1)
                pool.tensor_tensor(ln_rstd[:, :], ln_var[:, :], mhalf[:, :], op=ALU.pow).then_inc(ln_rstd_ok, 1)
                wait(pool, ln_rstd_ok, it, 2, e + 1)
                pool.tensor_tensor(a, a, lnr_b, op=ALU.mult).then_inc(ln_normed, 1)
                wait(pool, xhi_done, it, 2, e + 1)
                lo = xs[:, e, :, :, C:2 * C - 1].rearrange("p t s c -> p s t c")
                hi = xs[:, e, :, :, 0:C - 1].rearrange("p t s c -> p s t c")
                pool.tensor_tensor(lo, a[:, :, 0:C - 1].rearrange("p (s t) c -> p s t c", t=T), hi,
                                   op=ALU.subtract).then_inc(xlo_done, 1)

            def residual(it, e):
                r = ob[:, e, :, :, :].rearrange("p s t c -> p (s t) c")
                wait(pool, res_load[e], it, 16, 16)
                pool.tensor_tensor(r, r, bo_b, op=ALU.add).then_inc(res_ready, 1)

            normalise(0, 0)
            normalise(0, 1)
            loop_start[0] = 1
            with pool.Fori(1, NG // 2) as it:
                for e in range(2):
                    normalise(it, e)
                    residual(it - 1, e)
            loop_start[0] = 0
            residual(NG // 2 - 1, 0)
            residual(NG // 2 - 1, 1)

        @block.scalar
        def _(act):
            def deviation(t):
                act.wait_ge(zvar_ready, t + 1)
                act.activation(zq[:, 1, :], zq[:, 0, :], ACT.Sqrt).then_inc(zstd_ready, 1)

            def exponentials(t, half):
                act.wait_ge(soft_in, 2 * t + half + 1)
                for h in range(4 * half, 4 * half + 4):
                    act.activation(lg[:, t, h, :], lg[:, t, h, :], ACT.Exp, bias=nmax[:, h:h + 1],
                                   accum_out=esum[:, h:h + 1]).then_inc(soft_exp, 1)

            def weights_hi(t, half):
                for k in range(T):
                    w = (2 * t + half) * T + k
                    act.wait_ge(wt_pe, w + 1)
                    act.activation(wth[:, k, 4 * half:4 * half + 4, t * P:(t + 1) * P],
                                   ps_w[w % 2][:, :].rearrange("p (h q) -> p h q", h=4), ACT.Copy)\
                       .then_inc(wh_sb, 1)

            for t in range(T):
                def turn(i, first, t=t):
                    for b in range(ITER + 1):
                        n = t * QT_LOOPS * ITER + b
                        if b < ITER:
                            wait(act, lg_pe, i, ITER, n - 1)
                            for j in range(4):
                                wait(act, zt_pe, i, 4 * ITER, 4 * n + j + 1)
                                act.activation(ztr[:, b % 2, j, :], bank[j][:, :], ACT.Copy).then_inc(zt_sb, 1)
                        if b:
                            wait(act, lg_pe, i, ITER, n)
                            wait(act, bk_pe, i, ITER, n - 1)
                            act.activation(lraw[:, :], ps_lg[:, :], ACT.Copy).then_inc(lg_sb, 1)
                        if first and t:
                            if b == 0:
                                deviation(t - 1)
                            if b in (4, 5):
                                exponentials(t - 1, b - 4)
                            if b == 6:
                                weights_hi(t - 1, 0)
                                weights_hi(t - 1, 1)

                passes(act, turn)

            def square(m):
                act.activation(sq, xa[:, m % 2, :, :], ACT.Square).then_inc(ln_squared, 1)

            def store_hi(m):
                act.activation(xs[:, m % 2, :, :, 0:C - 1].rearrange("p t s c -> p s t c"),
                               xa[:, m % 2, :, 0:C - 1].rearrange("p (s t) c -> p s t c", t=T), ACT.Copy)\
                   .then_inc(xhi_done, 1)

            act.wait_ge(gn_var, 1)
            act.activation(gn[:, 5, :], gn[:, 4, :], ACT.Sqrt).then_inc(gn_std, 1)
            deviation(T - 1)
            exponentials(T - 1, 0)
            act.wait_ge(ln_centred, 1)
            square(0)
            exponentials(T - 1, 1)
            weights_hi(T - 1, 0)
            act.wait_ge(ln_normed, 1)
            store_hi(0)
            weights_hi(T - 1, 1)

            def step(it, c):
                two = lambda off: (off % PERIOD) // PAIRS
                if exists(it, c, 12):
                    q = c + 12
                    t, sp_ = q % PAIRS // 4, q % 4
                    wait(act, v_pe, it, PERIOD, q + 1)
                    if q % PAIRS == 0:
                        wait(act, o_pe, it, PERIOD, q - PAIRS)
                    act.activation(vh[:, two(q), t, :, 2 * sp_:2 * sp_ + 2, :].rearrange("p h s c -> p s h c"),
                                   ps_v[q % 2][:, :].rearrange("p (s h c) -> p s h c", s=2, h=H), ACT.Copy)\
                       .then_inc(vh_sb, 1)
                if exists(it, c, 4):
                    q = c + 4
                    wait(act, g_pe, it, PERIOD, q + 1)
                    if q % 4 == 0:
                        wait(act, gated_sb, it, PERIOD, q - 4)
                    act.activation(gate[:, q // 4 % 2, 2 * (q % 4):2 * (q % 4) + 2, :]
                                   .rearrange("p s n -> p (s n)"), ps_g[:, :], ACT.Sigmoid,
                                   scale=wback[:, 1:2]).then_inc(g_sb, 1)
                if exists(it, c, 0):
                    q, f, hp = c, c // 4, c % 4
                    wait(act, gated_sb, it, PERIOD, q + 1)
                    if hp % 2 == 0:
                        wait(act, gt_turn[f % 2][hp // 2], it, 48, 16 * (f // 2))
                    act.activation(gh[:, f % 2, hp // 2, 0, :, hp % 2 * C:(hp % 2 + 1) * C],
                                   gated[:, q % 2, :, :], ACT.Copy).then_inc(ghi_sb, 1)
                m, at = (c + 10) // PAIRS + 1, (c + 10) % PAIRS
                if at == 0 and exists(it, c, 22):
                    wait(act, ln_centred, it, 2, m + 1)
                    square(m)
                m, at = (c + 6) // PAIRS + 1, (c + 6) % PAIRS
                if at == 0 and exists(it, c, 18):
                    wait(act, ln_normed, it, 2, m + 1)
                    for t in range(T):
                        wait(act, xt_turn[m % 2][t], it, 16, 16 * (m // 2))
                    store_hi(m)

            steps(act, step)

        @block.vector
        def _(dve):
            links = [0]

            def link(ins):
                ins.then_inc(dlink, 1)
                links[0] += 1
                dve.wait_ge(dlink, links[0])

            dve.wait_ge(par_load, 12 * 16)
            dve.wait_ge(consts, 16)
            dve.tensor_tensor(centre_m[:, :], ident[:, :], mean_m[:, :], op=ALU.subtract)
            dve.tensor_copy(beta_sel[:, C - 1:C], vec[0:C, 3:4])
            dve.tensor_copy(beta_sel[:, 2 * C - 1:2 * C], vec[0:C, 3:4])
            dve.tensor_scalar(wvg_g[:, :], wvg[:, :], vec[0:C, 2:3], None, ALU.mult)
            dve.tensor_scalar(wz_g[:, :], wz[:, :], vec[:, 0:1], None, ALU.mult)
            dve.tensor_scalar(beta_zb[:, :], mean_m[:, :], float(P), vec[:, 1:2], ALU.mult, ALU.mult)\
               .then_inc(prep_w, 1)
            dve.wait_ge(wprod, 1)
            dve.tensor_copy(wzc[:, 0:H], bank[7][:, 0:H])
            dve.tensor_copy(bzo[:, :], bank[7][:, H:2 * H + C])
            link(dve.tensor_copy(wfull[:, :], bank[6][:, :]))
            for i in range(2):
                dve.tensor_reduce(wmax[:, i:i + 1], wfull[:, i * D:(i + 1) * D], axis=AX_X, op=ALU.max,
                                  apply_absolute_value=True)
            dve.tensor_reduce(wmax[:, 2:3], wo[:, :, :].rearrange("p a n -> p (a n)"), axis=AX_X, op=ALU.max,
                              apply_absolute_value=True).then_inc(wmax_ready, 1)
            dve.wait_ge(wmaxa_ready, 1)
            link(dve.tensor_scalar(wmaxa[:, :], wmaxa[:, :], 1e-30, None, ALU.max))
            link(dve.tensor_scalar(wpow[:, :].bitcast(I32), wmaxa[:, :].bitcast(I32), 0x7F800000, None,
                                   ALU.bitwise_and))
            link(dve.reciprocal(wscale[:, :], wpow[:, :]))
            dve.tensor_scalar(wback[:, :], wpow[:, :], 1.0 / W_TARGET, None, ALU.mult)
            link(dve.tensor_scalar(wscale[:, :], wscale[:, :], W_TARGET, None, ALU.mult))
            dve.tensor_tensor(oscale[:, :], wback[:, 0:1], wback[:, 2:3], op=ALU.mult)
            for i in range(2):
                dve.tensor_scalar(wvg_hi[:, i * D:(i + 1) * D], wfull[:, i * D:(i + 1) * D], wscale[:, i:i + 1],
                                  None, ALU.mult)
            link(dve.tensor_scalar(wo_hi[:, :, :], wo[:, :, :], wscale[:, 2:3], None, ALU.mult))
            for i in range(2):
                dve.scalar_tensor_tensor(wvg_lo[:, i * D:(i + 1) * D], wfull[:, i * D:(i + 1) * D],
                                         wscale[:, i:i + 1], wvg_hi[:, i * D:(i + 1) * D], ALU.mult, ALU.subtract)
            dve.scalar_tensor_tensor(wo_lo[:, :, :], wo[:, :, :], wscale[:, 2:3], wo_hi[:, :, :],
                                     ALU.mult, ALU.subtract).then_inc(w_ready, 1)

            def variance(t):
                dve.wait_ge(zst_done, (t + 1) * QT_LOOPS * ITER)
                dve.tensor_scalar(zq[:, 0, :], zst[:, :, 2], 1.0 / CZ, EPS, ALU.mult, ALU.add)\
                   .then_inc(zvar_ready, 1)
                dve.wait_ge(zvar_ready, t + 1)

            def scale_rows(t):
                dve.wait_ge(mask_load, 16 * (t + 1))
                dve.tensor_scalar(mk[:, :], mk[:, :], -1.0, INF, ALU.add, ALU.mult)
                dve.wait_ge(zstd_ready, t + 1)
                dve.reciprocal(zq[:, 0, :], zq[:, 1, :]).then_inc(zinv_ready, 1)

            def biased(t, half):
                hs = slice(4 * half, 4 * half + 4)
                dve.wait_ge(zinv_ready, t + 1)
                if t < T - 1:
                    dve.wait_ge(lg_scaled, 2 * t + half + 1)
                else:
                    dve.wait_ge(bk_sb, NB)
                    link(divide_std(dve, t, half))
                for h in range(4 * half, 4 * half + 4):
                    last = dve.scalar_tensor_tensor(lg[:, t, h, :], lg[:, t, h, :], bzo[:, h:h + 1], mk[:, :],
                                                    ALU.add, ALU.add)
                link(last)
                dve.tensor_reduce(nmax[:, hs], lg[:, t, hs, :], axis=AX_X, op=ALU.max, negate=True)\
                   .then_inc(soft_in, 1)

            def normalised(t, half):
                hs = slice(4 * half, 4 * half + 4)
                dve.wait_ge(soft_exp, H * t + 4 * half + 4)
                if t:
                    dve.wait_ge(soft_w, 2 * t)
                link(dve.reciprocal(einv[:, hs], esum[:, hs]))
                last = dve.tensor_scalar(einv[:, hs], einv[:, hs], W_SCALE, None, ALU.mult)
                last.then_inc(esum_inv, 1)
                if t == T - 1:
                    dve.wait_ge(esum_inv, 2 * t + half + 1)
                    divide_sum(dve, t, half).then_inc(soft_w, 1)

            def weights_lo(t, half):
                for k in range(T):
                    w = (2 * t + half) * T + k
                    dve.wait_ge(wh_sb, w + 1)
                    at = (slice(None), k, slice(4 * half, 4 * half + 4), slice(t * P, (t + 1) * P))
                    dve.tensor_tensor(wtl[at], ps_w[w % 2][:, :].rearrange("p (h q) -> p h q", h=4), wth[at],
                                      op=ALU.subtract).then_inc(wl_sb, 1)

            for t in range(T):
                def measure(i, first, t=t):
                    def keep_logits(b):
                        n = t * QT_LOOPS * ITER + b
                        wait(dve, bk_pe, i, ITER, n + 1)
                        dve.tensor_copy(
                            lg[:, t, :, bass.ds(i * (ITER * ZB) + b * ZB, ZB)]
                            .rearrange("p h (j k) -> p h j k", k=4),
                            ps_back[:, :].rearrange("p (k j h) -> p h j k", k=4, j=4)[:, 0:H, :, :])\
                           .then_inc(bk_sb, 1)

                    for b in range(ITER):
                        if first and t:
                            if b == 0:
                                variance(t - 1)
                            if b == 1:
                                scale_rows(t - 1)
                            if b in (3, 4):
                                biased(t - 1, b - 3)
                            if b == 5:
                                normalised(t - 1, 0)
                        n = t * QT_LOOPS * ITER + b
                        wait(dve, z_load[b], i, 16, 16 * (n // ITER + 1))
                        for k in range(0, ZB, 2):
                            last = dve.bn_stats(zst[:, bass.ds(i * (ITER * ZB) + (b * ZB + k), 2), :]
                                                .rearrange("p k s -> p (k s)"),
                                                z_buf[b][:, k:k + 2, :].rearrange("p k c -> p c k"))
                        last.then_inc(zst_done, 1)
                        if b >= 2:
                            keep_logits(b - 2)
                    m = t * QT_LOOPS
                    keep_logits(ITER - 2)
                    if first and t:
                        normalised(t - 1, 1)
                    wait(dve, xc_load, i, 16, 16 * (m + 1))
                    for g in range(GRP):
                        last = dve.bn_stats(xst[:, g, bass.ds(i + m, 1), :].rearrange("p x s -> p (x s)"),
                                            xch[:, :, g, :])
                        if g == GRP // 2:
                            keep_logits(ITER - 1)
                        if first and t and g in (12, 24):
                            weights_lo(t - 1, g // 12 - 1)
                    last.then_inc(xst_done, 1)

                passes(dve, measure)

            cnt = 2 * NX
            dve.wait_ge(xst_done, NX)
            link(dve.tensor_reduce(gn[:, 0, :], xst3[:, :, :, 1], axis=AX_X, op=ALU.add))
            link(dve.tensor_scalar(gn[:, 0, :], gn[:, 0, :], 1.0 / cnt, None, ALU.mult))
            nop = dve.tensor_copy(gn[:, 1, :], gn[:, 0, :])
            nop.then_inc(gn_part, 1)
            link(dve.tensor_tensor(tmp, xst3[:, :, :, 1], gn[:, 0, :].unsqueeze(2).broadcast_to([P, GRP, cnt]),
                                   op=ALU.subtract))
            link(dve.tensor_tensor(tmp, tmp, tmp, op=ALU.mult))
            link(dve.tensor_reduce(gn[:, 2, :], tmp, axis=AX_X, op=ALU.add))
            link(dve.tensor_reduce(gn[:, 3, :], xst3[:, :, :, 2], axis=AX_X, op=ALU.add))
            link(dve.scalar_tensor_tensor(gn[:, 2, :], gn[:, 2, :], float(XB), gn[:, 3, :], ALU.mult, ALU.add))
            dve.wait_ge(gn_mm, 1)
            for e in range(2):
                dve.tensor_copy(gn_mean[:, :].rearrange("p (g e) -> p g e", e=2)[:, :, e], ps_w[1][:, 0:GRP])
            link(dve.tensor_tensor(gn[:, 3, :], gn[:, 0, :], ps_w[1][:, 0:GRP], op=ALU.subtract))
            link(dve.tensor_tensor(gn[:, 3, :], gn[:, 3, :], gn[:, 3, :], op=ALU.mult))
            dve.scalar_tensor_tensor(gn[:, 2, :], gn[:, 2, :], 1.0 / (cnt * XB), gn[:, 3, :],
                                     ALU.mult, ALU.add).then_inc(gn_part, 1)
            dve.wait_ge(gn_mm, 2)
            dve.tensor_scalar(gn[:, 4, :], ps_w[1][:, GRP:2 * GRP], EPS, None, ALU.add).then_inc(gn_var, 1)
            dve.wait_ge(gn_std, 1)
            link(dve.reciprocal(gn[:, 3, :], gn[:, 5, :]))
            for e in range(2):
                dve.tensor_copy(gn_rstd[:, :].rearrange("p (g e) -> p g e", e=2)[:, :, e], gn[:, 3, :])\
                   .then_inc(gn_ready, 1)

            def mean_of(m):
                dve.tensor_reduce(ln_sum[:, :], xa[:, m % 2, :, :], axis=AX_X, op=ALU.add).then_inc(ln_summed, 1)

            def variance_of(m):
                dve.tensor_reduce(ln_ssq[:, :], sq, axis=AX_X, op=ALU.add).then_inc(ln_ssummed, 1)

            def mean_out():
                dve.tensor_scalar(ln_mean[:, :], ln_sum[:, :], 1.0 / C, None, ALU.mult).then_inc(ln_mean_ok, 1)

            def variance_out():
                dve.tensor_scalar(ln_var[:, :], ln_ssq[:, :], 1.0 / C, EPS, ALU.mult, ALU.add)\
                   .then_inc(ln_var_ok, 1)

            variance(T - 1)
            scale_rows(T - 1)
            biased(T - 1, 0)
            dve.wait_ge(ln_scaled, 1)
            mean_of(0)
            dve.wait_ge(ln_summed, 1)
            mean_out()
            biased(T - 1, 1)
            dve.wait_ge(ln_squared, 1)
            variance_of(0)
            dve.wait_ge(ln_ssummed, 1)
            variance_out()
            normalised(T - 1, 0)
            normalised(T - 1, 1)
            weights_lo(T - 1, 0)
            weights_lo(T - 1, 1)

            def step(it, c):
                two = lambda off: (off % PERIOD) // PAIRS
                if exists(it, c, -1):
                    q, f, hp = c - 1, (c - 1) // 4, (c - 1) % 4
                    wait(dve, ghi_sb, it, PERIOD, q + 1)
                    cols = slice(hp % 2 * C, (hp % 2 + 1) * C)
                    dve.tensor_tensor(gh[:, f % 2, hp // 2, 1, :, cols], gated[:, q % 2, :, :],
                                      gh[:, f % 2, hp // 2, 0, :, cols], op=ALU.subtract).then_inc(glo_sb, 1)
                if exists(it, c, 12):
                    q = c + 12
                    t, sp_ = q % PAIRS // 4, q % 4
                    wait(dve, vh_sb, it, PERIOD, q + 1)
                    view = lambda v: v[:, two(q), t, :, 2 * sp_:2 * sp_ + 2, :].rearrange("p h s c -> p s h c")
                    dve.tensor_tensor(view(vl), ps_v[q % 2][:, :].rearrange("p (s h c) -> p s h c", s=2, h=H), view(vh),
                                      op=ALU.subtract).then_inc(vl_sb, 1)
                if exists(it, c, 0):
                    q, f, hp = c, c // 4, c % 4
                    wait(dve, o_pe, it, PERIOD, q + 1)
                    if hp == 0:
                        wait(dve, g_sb, it, PERIOD, q + 4)
                    wait(dve, glo_sb, it, PERIOD, q - 1)
                    heads = slice(2 * hp * (D // H), (2 * hp + 2) * (D // H))
                    dve.scalar_tensor_tensor(gated[:, q % 2, :, :],
                                             ps_o[q % 2][:, :].rearrange("p (s n) -> p s n", s=R), 1.0 / W_SCALE,
                                             gate[:, f % 2, :, heads], ALU.mult, ALU.mult).then_inc(gated_sb, 1)
                if c % 4 == 0 and exists(it, c, -12):
                    f = c // 4 - 3
                    t, n = f % T, f // T
                    wait(dve, p_pe, it, PERIOD, 4 * f + 4)
                    wait(dve, res_ready, it, 2, n + 1)
                    o = ob[:, n % 2, :, t, :]
                    dve.scalar_tensor_tensor(o, ps_p[f % 2][:, :].rearrange("p (s c) -> p s c", s=R), oscale[:, 0:1], o,
                                             ALU.mult, ALU.add).then_inc(fin_sb, 1)
                m, at = c // PAIRS + 2, c % PAIRS
                if at == 0 and exists(it, c, 24):
                    wait(dve, ln_scaled, it, 2, m + 1)
                    mean_of(m)
                    wait(dve, ln_summed, it, 2, m + 1)
                    mean_out()
                m, at = (c + 9) // PAIRS + 1, (c + 9) % PAIRS
                if at == 0 and exists(it, c, 21):
                    wait(dve, ln_squared, it, 2, m + 1)
                    variance_of(m)
                    wait(dve, ln_ssummed, it, 2, m + 1)
                    variance_out()

            steps(dve, step)

        @block.tensor
        def _(pe):
            mm = nc.tensor.matmul
            pe.wait_ge(consts, 16)
            pe.wait_ge(prep_w, 1)
            mm(bank[6][:, :], drop_m[:, :], wvg_g[:, :], start=True, stop=False)
            mm(bank[6][:, :], beta_sel[:, :], wvg[:, :], start=False, stop=False)
            mm(bank[6][:, :], bias_sel[:, :], bvg[:, :], start=False, stop=True)
            mm(bank[7][:, 0:H], centre_m[:, :], wz_g[:, :], start=True, stop=True)
            mm(bank[7][:, H:2 * H], beta_zb[:, :], wz[:, :], start=True, stop=False)
            mm(bank[7][:, H:2 * H], ones_row[:, :], brow[:, 0:H], start=False, stop=True)
            mm(bank[7][:, 2 * H:2 * H + C], ones_row[:, :], brow[:, H:H + C], start=True, stop=True)\
                .then_inc(wprod, 1)
            pe.wait_ge(w_ready, 1)

            def turn_weights(t, half):
                pe.wait_ge(soft_w, 2 * t + half + 1)
                for k in range(T):
                    w = (2 * t + half) * T + k
                    if w >= 2:
                        pe.wait_ge(wl_sb, w - 1)
                    for j in range(4):
                        blk = lg[:, t, 4 * half + j, :].rearrange("p (k t) -> p t k", t=T)[:, k, :]
                        last = nc.tensor.transpose(ps_w[w % 2][:, j * P:(j + 1) * P], blk, ident[:, :])
                    last.then_inc(wt_pe, 1)

            for t in range(T):
                def logits(i, first, t=t):
                    for b in range(ITER + 2):
                        n = t * QT_LOOPS * ITER + b
                        if b < ITER:
                            wait(pe, z_load[b], i, 16, 16 * (n // ITER + 1))
                            for j in range(4):
                                wait(pe, zt_sb, i, 4 * ITER, 4 * n + j - 3)
                                for k in range(4):
                                    last = nc.tensor.transpose(bank[j][:, k * P:(k + 1) * P],
                                                               z_buf[b][:, 4 * j + k, :], ident[:, :])
                                last.then_inc(zt_pe, 1)
                        if b >= 2:
                            wait(pe, lg_sb, i, ITER, n - 1)
                            wait(pe, bk_sb, i, ITER, n - 2)
                            for k in range(4):
                                last = nc.tensor.transpose(ps_back[:, k * P:(k + 1) * P],
                                                           lraw[:, k * P:(k + 1) * P], ident[:, :])
                            last.then_inc(bk_pe, 1)
                        if 1 <= b <= ITER:
                            wait(pe, zt_sb, i, 4 * ITER, 4 * n)
                            wait(pe, lg_sb, i, ITER, n - 1)
                            for j in range(4):
                                last = mm(ps_lg[32 * j:32 * j + 32, :], wzc[:, :], ztr[:, (b - 1) % 2, j, :],
                                          start=True, stop=True)
                            last.then_inc(lg_pe, 1)
                        if first and t and b in (6, 7):
                            turn_weights(t - 1, b - 6)

                passes(pe, logits)
            pe.wait_ge(wl_sb, 2 * T * (T - 1))
            for i, src in enumerate((1, 2)):
                pe.wait_ge(gn_part, i + 1)
                mm(ps_w[1][:, i * GRP:(i + 1) * GRP], mean_m[:, :], gn[:, src, :], start=True, stop=True)\
                    .then_inc(gn_mm, 1)

            pe.wait_ge(gn_ready, 2)
            turn_weights(T - 1, 0)
            turn_weights(T - 1, 1)

            pe.wait_ge(bk_sb, NB)

            def step(it, c):
                two = lambda off: (off % PERIOD) // PAIRS

                def average(hh):
                    q, t, h = c, c % PAIRS // 4, 2 * (c % 4) + hh
                    for k in range(T):
                        w_hi, w_lo = wth[:, k, h, t * P:(t + 1) * P], wtl[:, k, h, t * P:(t + 1) * P]
                        v_hi, v_lo = vh[:, two(q), k, h, :, :], vl[:, two(q), k, h, :, :]
                        o = ps_o[q % 2][:, :].rearrange("p (s h c) -> p h s c", s=R, h=2)[:, hh, :, :]
                        mm(o, w_hi, v_hi, start=k == 0, stop=False)
                        mm(o, w_hi, v_lo, start=False, stop=False)
                        last = mm(o, w_lo, v_hi, start=False, stop=k == T - 1)
                    if hh == 1:
                        last.then_inc(o_pe, 1)

                def project(it, q, ps, done, free, buffers, off):
                    if not exists(it, q, 0):
                        return
                    if q % 4 == 0:
                        wait(pe, xt_turn[two(q)][q % PAIRS // 4], it, 16, 16 * (q // PERIOD + 1))
                    wait(pe, free, it, PERIOD, q - buffers + 1)
                    for s in range(2):
                        x_t = xt[:, two(q), q % PAIRS // 4, 2 * (q % 4) + s, :]
                        mm(ps[:, s * D:(s + 1) * D], x_t, wvg_hi[:, off:off + D], start=True, stop=False)
                        last = mm(ps[:, s * D:(s + 1) * D], x_t, wvg_lo[:, off:off + D], start=False, stop=True)
                    last.then_inc(done, 1)

                if exists(it, c, 0):
                    wait(pe, gated_sb, it, PERIOD, c - 1)
                    if c % PAIRS == 0:
                        wait(pe, vh_sb, it, PERIOD, c + PAIRS)
                        wait(pe, vl_sb, it, PERIOD, c + PAIRS)
                    average(0)
                project(it, c + 12, ps_v[c % 2], v_pe, vl_sb, 2, 0)
                project(it, c + 4, ps_g, g_pe, g_sb, 1, D)
                if exists(it, c, 0):
                    average(1)
                if exists(it, c, -8):
                    q, f = c - 8, (c - 8) // 4
                    if q % 4 == 0:
                        for a in range(2):
                            wait(pe, gt_turn[f % 2][a], it, 48, 16 * (f // 2 + 1))
                        wait(pe, fin_sb, it, 2 * T, f - 1)
                    for row in range(2 * (q % 4), 2 * (q % 4) + 2):
                        o = ps_p[f % 2][:, row * C:(row + 1) * C]
                        for a in range(2):
                            g_hi, g_lo = gt[:, f % 3, a, 0, row, :], gt[:, f % 3, a, 1, row, :]
                            mm(o, g_hi, wo_hi[:, a, :], start=a == 0, stop=False)
                            mm(o, g_hi, wo_lo[:, a, :], start=False, stop=False)
                            last = mm(o, g_lo, wo_hi[:, a, :], start=False, stop=a == 1)
                    last.then_inc(p_pe, 1)

            steps(pe, step)


_INS = ["x"] + ["L0_conv_" + n for n in ("z", "mask", "gamma_m", "beta_m", "gamma_z", "beta_z", "w_z", "b_z",
                                         "w_v", "b_v", "w_g", "b_g", "w_o", "b_o")]


def kernel(**inputs):
    import numpy as np
    import concourse.bacc as bacc
    from concourse.bass_utils import run_bass_kernel_spmd

    nc = bacc.Bacc("TRN2", target_bir_lowering=False, num_devices=1)
    arrays, args = {}, []
    for name in _INS:
        a = np.ascontiguousarray(inputs[name])
        arrays[f"in_{name}"] = a
        args.append(nc.dram_tensor(f"in_{name}", a.shape, mybir.dt.from_np(a.dtype), kind="ExternalInput").ap())
    args.append(nc.dram_tensor("out", arrays["in_x"].shape, F32, kind="ExternalOutput").ap())
    pair_weighted(nc, *args)
    return run_bass_kernel_spmd(nc, [arrays], core_ids=[0]).results[0]["out"]
```

```python
from contextlib import ExitStack

import concourse.bass as bass
from concourse import mybir

F32 = mybir.dt.float32
F16 = mybir.dt.float16
I32 = mybir.dt.int32
ALU = mybir.AluOpType
ACT = mybir.ActivationFunctionType
AX_X = mybir.AxisListType.X
ABSMAX = bass.bass_isa.ReduceOp.absmax

P = 128
EPS = 1e-5
INF = 1e9
W_SCALE = 2.0 ** 14
W_TARGET = 2.0 ** 7

R = 8
PAIRS = 12
PERIOD = 2 * PAIRS
FIRST = 24
AHEAD = 12
AFTER = 10


def pair_weighted(nc, x, z, mask, gamma_m, beta_m, gamma_z, beta_z, w_z, b_z, w_v, b_v, w_g, b_g, w_o, b_o, out):
    _, S, N, C = x.shape
    CZ = z.shape[-1]
    H = w_z.shape[-1]
    D = w_v.shape[-1]
    HC = D // H
    T = N // P
    NG = S // R
    STEPS = NG * PAIRS
    LOOPS = (STEPS - 41 - FIRST) // PERIOD
    TAIL = FIRST + LOOPS * PERIOD
    assert (T, C, CZ, H, D) == (3, 64, 128, 8, 256)

    ZB = 16
    ITER = 6
    QT_LOOPS = N // (ZB * ITER)
    NB = T * QT_LOOPS * ITER
    XB = 128
    NX = S * N // P // XB
    GRP = 32
    assert NX == T * QT_LOOPS
    BEFORE_X = 4

    x_rows = x.rearrange("o s (p t) c -> p (o s) (t c)", t=T)
    out_rows = out.rearrange("o s (p t) c -> p (o s) (t c)", t=T)
    x_flat = x.rearrange("o s n c -> (o s n c)").rearrange("(p f) -> p f", p=P)
    z_flat = z.rearrange("o (p t) k c -> p (o t k) c", t=T)
    mask_rows = mask.rearrange("o (p t) k -> p (o t) k", t=T)

    with ExitStack() as ctx:
        def sb(name, shape, dt):
            return ctx.enter_context(nc.sbuf_tensor(name, shape, dt))

        def sem(name):
            return ctx.enter_context(nc.semaphore(name))

        reg_x = sb("reg_x", [P, 6144], F32)
        reg_a = sb("reg_a", [P, 4608], F32)
        reg_v = sb("reg_v", [P, 12288], F32)
        reg_g = sb("reg_g", [P, 9216], F32)
        reg_o = sb("reg_o", [P, 3072], F32)
        reg_z = sb("reg_z", [P, 6144], F32)
        wth = sb("wth", [P, T, H, N], F16)
        reg_w = sb("reg_w", [P, 4608], F32)
        wtl = reg_w[:, :].bitcast(F16).rearrange("p (t h q) -> p t h q", t=T, h=H)
        xa = reg_x[:, 0:3072].rearrange("p (b r c) -> p b r c", b=2, c=C)
        xs = reg_x[:, 3072:6144].bitcast(F16).rearrange("p (b t s c) -> p b t s c", b=2, s=R, t=T)
        xt = reg_a[:, 0:3072].bitcast(F16).rearrange("p (b t s n) -> p b t s n", b=2, t=T, s=R)
        sq = reg_a[:, 3072:4608].rearrange("p (r c) -> p r c", c=C)
        vh = reg_v[:, 0:6144].bitcast(F16).rearrange("p (b t h s c) -> p b t h s c", b=2, t=T, h=H, s=R)
        vl = reg_v[:, 6144:12288].bitcast(F16).rearrange("p (b t h s c) -> p b t h s c", b=2, t=T, h=H, s=R)
        gate = reg_g[:, 0:4096].rearrange("p (b s n) -> p b s n", b=2, s=R)
        gated = reg_g[:, 4096:5120].rearrange("p (b s n) -> p b s n", b=2, s=R)
        gh = reg_g[:, 5120:9216].bitcast(F16).rearrange("p (b a l s n) -> p b a l s n", b=2, a=2, l=2, s=R)
        gt = reg_z[:, :].bitcast(F16).rearrange("p (b a l s n) -> p b a l s n", b=3, a=2, l=2, s=R)
        ob = reg_o[:, :].rearrange("p (b s t c) -> p b s t c", b=2, s=R, t=T)
        xst = reg_a[:, 0:GRP * NX * 6].rearrange("p (g x s) -> p g x s", g=GRP, x=NX)
        xst3 = reg_a[:, 0:GRP * NX * 6].rearrange("p (g x s) -> p g x s", g=GRP, s=3)
        xch = reg_v[:, 0:XB * C].rearrange("p (n g e) -> p n g e", n=XB, g=GRP)
        ztr = reg_v[:, 8192:12288].rearrange("p (b j n) -> p b j n", b=2, j=4)
        lg = reg_g[:, :].rearrange("p (t h k) -> p t h k", t=T, h=H)
        zst = reg_o[:, 0:3 * N].rearrange("p (k s) -> p k s", s=3)
        zrs = reg_o[:, 2304:2304 + N]
        zvar = reg_o[:, 2304 + N:2304 + N + 2 * ZB].rearrange("p (b k) -> p b k", b=2)
        wvg = reg_w[0:C, 0:512]
        wvg_g = reg_w[0:C, 512:1024]
        bvg = reg_w[0:1, 1024:1536]
        wfull = reg_w[:, 1536:2048]
        centre_m = reg_w[:, 2048:2176]
        drop_m = reg_w[0:C, 2176:2304]
        beta_sel = reg_w[0:C, 2304:2432]
        bias_sel = reg_w[0:1, 2432:2560]
        ones_row = reg_w[0:1, 2560:2688]
        beta_zb = reg_w[:, 2688:2816]
        wo = reg_w[:, 3712:3840].rearrange("p (a n) -> p a n", a=2)
        wz = reg_w[:, 3840:3848]
        wz_g = reg_w[:, 3848:3856]
        z_buf = [reg[:, i * ZB * CZ:(i + 1) * ZB * CZ].rearrange("p (k c) -> p k c", c=CZ)
                 for reg in (reg_x, reg_z) for i in range(3)]
        lraw = sb("lraw", [P, 512], F32)
        mk = sb("mk", [P, N], F32)
        tmp = reg_z[:, 0:GRP * NX * 2].rearrange("p (g x) -> p g x", g=GRP)

        gn = reg_z[:, 1024:1024 + 6 * GRP].rearrange("p (a g) -> p a g", a=6)

        ident = sb("ident", [P, P], F32)
        mean_m = sb("mean_m", [P, P], F32)
        wvg_hi = sb("wvg_hi", [P, 2 * D], F16)
        wvg_lo = sb("wvg_lo", [P, 2 * D], F16)
        wo_hi = sb("wo_hi", [P, 2, C], F16)
        wo_lo = sb("wo_lo", [P, 2, C], F16)
        wzc = sb("wzc", [P, 32], F32)
        vec = sb("vec", [P, 4], F32)
        brow = sb("brow", [1, H + C], F32)
        bzo = sb("bzo", [P, H + C], F32)
        wmax = sb("wmax", [P, 3], F32)
        wmaxa = sb("wmaxa", [P, 3], F32)
        wpow = sb("wpow", [P, 3], F32)
        wscale = sb("wscale", [P, 3], F32)
        wback = sb("wback", [P, 3], F32)
        oscale = sb("oscale", [P, 1], F32)
        mhalf = sb("mhalf", [P, R * T], F32)
        eps_c = sb("eps_c", [P, 1], F32)
        eps_z = sb("eps_z", [P, ZB], F32)
        gn_mean = sb("gn_mean", [P, C], F32)
        gn_rstd = sb("gn_rstd", [P, C], F32)
        ln_sum = sb("ln_sum", [P, R * T], F32)
        ln_mean = sb("ln_mean", [P, R * T], F32)
        ln_ssq = sb("ln_ssq", [P, R * T], F32)
        ln_var = sb("ln_var", [P, R * T], F32)
        ln_rstd = sb("ln_rstd", [P, R * T], F32)
        nmax = sb("nmax", [P, H], F32)
        esum = sb("esum", [P, H], F32)
        einv = sb("einv", [P, H], F32)

        bank = [ctx.enter_context(nc.psum_tensor(f"bank{i}", [P, 512], F32)) for i in range(8)]
        ps_o = bank[0:2]
        ps_v, ps_g, ps_p = bank[2:4], bank[5], bank[6:8]
        ps_lg, ps_back, ps_w = bank[4], bank[5], bank[6:8]

        par_load = sem("par_load")
        mask_load = sem("mask_load")
        z_load = [sem(f"z_load{i}") for i in range(6)]
        xc_load = sem("xc_load")
        xa_load = [sem(f"xa_load{i}") for i in range(2)]
        res_load = [sem(f"res_load{i}") for i in range(2)]
        out_store = [sem(f"out_store{i}") for i in range(2)]
        consts = sem("consts")
        dlink = sem("dlink")
        prep_w = sem("prep_w")
        wprod = sem("wprod")
        wmax_ready = sem("wmax_ready")
        wmaxa_ready = sem("wmaxa_ready")
        w_ready = sem("w_ready")
        zt_pe = sem("zt_pe")
        zt_sb = sem("zt_sb")
        lg_pe = sem("lg_pe")
        lg_sb = sem("lg_sb")
        bk_pe = sem("bk_pe")
        bk_sb = sem("bk_sb")
        zst_done = sem("zst_done")
        xst_done = sem("xst_done")
        zvar_ready = sem("zvar_ready")
        zrs_ready = sem("zrs_ready")
        zlast_var = sem("zlast_var")
        zlast_std = sem("zlast_std")
        lg_scaled = sem("lg_scaled")
        mask_ready = sem("mask_ready")
        soft_in = sem("soft_in")
        esum_inv = sem("esum_inv")
        soft_exp = sem("soft_exp")
        soft_w = sem("soft_w")
        wt_pe = sem("wt_pe")
        wh_sb = sem("wh_sb")
        wl_sb = sem("wl_sb")
        gn_part = sem("gn_part")
        gn_mm = sem("gn_mm")
        gn_var = sem("gn_var")
        gn_std = sem("gn_std")
        gn_ready = sem("gn_ready")
        ln_shifted = sem("ln_shifted")
        ln_scaled = sem("ln_scaled")
        ln_summed = sem("ln_summed")
        ln_mean_ok = sem("ln_mean_ok")
        ln_centred = sem("ln_centred")
        ln_squared = sem("ln_squared")
        ln_ssummed = sem("ln_ssummed")
        ln_var_ok = sem("ln_var_ok")
        ln_rstd_ok = sem("ln_rstd_ok")
        ln_normed = sem("ln_normed")
        xhi_done = sem("xhi_done")
        xlo_done = sem("xlo_done")
        xs_const = sem("xs_const")
        res_ready = sem("res_ready")
        xt_turn = [[sem(f"xt_turn{b}{t}") for t in range(T)] for b in range(2)]
        v_pe = sem("v_pe")
        vh_sb = sem("vh_sb")
        vl_sb = sem("vl_sb")
        g_pe = sem("g_pe")
        g_sb = sem("g_sb")
        o_pe = sem("o_pe")
        gated_sb = sem("gated_sb")
        ghi_sb = sem("ghi_sb")
        glo_sb = sem("glo_sb")
        turn_next = sem("turn_next")
        gt_turn = [[sem(f"gt_turn{b}{a}") for a in range(2)] for b in range(2)]
        p_pe = sem("p_pe")
        fin_sb = sem("fin_sb")

        block = ctx.enter_context(nc.Block())

        loop_start = [0]

        def passes(eng, t, body):
            ends = t == T - 1
            body(0, True, False)
            loop_start[0] = 1
            with eng.Fori(1, QT_LOOPS - ends) as i:
                body(i, False, False)
            loop_start[0] = 0
            if ends:
                body(QT_LOOPS - 1, False, True)

        def steps(eng, step):
            for c in range(-AHEAD, FIRST):
                step(0, c)
            with eng.Fori(0, LOOPS) as it:
                for c in range(FIRST, FIRST + PERIOD):
                    step(it, c)
            for c in range(FIRST, FIRST + STEPS + AFTER - TAIL):
                step(LOOPS, c)

        def exists(it, c, shift):
            return not isinstance(it, int) or 0 <= PERIOD * it + c + shift < STEPS

        def ln_group(c, ahead, ahead_1):
            if c == -ahead_1:
                return 1
            return (c + ahead) // PAIRS + 1 if c + ahead >= PAIRS and (c + ahead) % PAIRS == 0 else None

        def wait(eng, s, it, per, n):
            if isinstance(it, int):
                if per * it + n > 0:
                    eng.wait_ge(s, per * it + n)
            else:
                assert per * loop_start[0] + n > 0
                eng.wait_ge(s, it * per + n)

        def divide_std(eng, t, half):
            hs = slice(4 * half, 4 * half + 4)
            return eng.tensor_tensor(lg[:, t, hs, :], lg[:, t, hs, :],
                                     zrs.unsqueeze(1).broadcast_to([P, 4, N]), op=ALU.mult)

        def divide_sum(eng, t, half):
            hs = slice(4 * half, 4 * half + 4)
            return eng.tensor_tensor(lg[:, t, hs, :], lg[:, t, hs, :],
                                     einv[:, hs].unsqueeze(2).broadcast_to([P, 4, N]), op=ALU.mult)

        @block.sync
        def _(sp):
            sp.dma_start(wvg[:, 0:D], w_v).then_inc(par_load, 16)
            sp.dma_start(wvg[:, D:2 * D], w_g).then_inc(par_load, 16)
            sp.dma_start(bvg[:, 0:D], b_v.rearrange("(a n) -> a n", a=1)).then_inc(par_load, 16)
            sp.dma_start(bvg[:, D:2 * D], b_g.rearrange("(a n) -> a n", a=1)).then_inc(par_load, 16)
            sp.dma_start(wo[:, :, :], w_o.rearrange("(a p) n -> p a n", a=2)).then_inc(par_load, 16)
            sp.dma_start(wz[:, :], w_z).then_inc(par_load, 16)
            sp.dma_start(vec[:, 0:1], gamma_z.rearrange("(p a) -> p a", a=1)).then_inc(par_load, 16)
            sp.dma_start(vec[:, 1:2], beta_z.rearrange("(p a) -> p a", a=1)).then_inc(par_load, 16)
            sp.dma_start(vec[0:C, 2:3], gamma_m.rearrange("(p a) -> p a", a=1)).then_inc(par_load, 16)
            sp.dma_start(vec[0:C, 3:4], beta_m.rearrange("(p a) -> p a", a=1)).then_inc(par_load, 16)
            sp.dma_start(brow[:, 0:H], b_z.rearrange("(a n) -> a n", a=1)).then_inc(par_load, 16)
            sp.dma_start(brow[:, H:H + C], b_o.rearrange("(a n) -> a n", a=1)).then_inc(par_load, 16)
            def at(n, size):
                return n * size if isinstance(n, int) else sp.snap(n * size)

            def load_z(k, slot):
                sp.dma_start(z_buf[slot], z_flat[:, bass.ds(k, ZB), :]).then_inc(z_load[slot], 16)

            def load_chunk(f):
                sp.dma_start(xch.rearrange("p n g e -> p (n g e)"), x_flat[:, bass.ds(f, XB * C)])\
                  .then_inc(xc_load, 16)

            def feed(i):
                for b in range(ITER):
                    if b == BEFORE_X:
                        f, taken = at(i + 1, XB * C), at(i + 1, 1)
                        sp.wait_ge(xst_done, taken)
                        load_chunk(f)
                    k = at((i + 1) * ITER + b, ZB)
                    turned, measured = at(i * ITER + (b + 1), 4), at(i * ITER + (b + 1), 1)
                    sp.wait_ge(zt_pe, turned)
                    sp.wait_ge(zst_done, measured)
                    load_z(k, b)

            for n in range(ITER):
                if n == BEFORE_X:
                    load_chunk(0)
                load_z(n * ZB, n)
            with sp.Fori(0, T * QT_LOOPS - 1) as i:
                feed(i)

            def load_x(row, slot):
                sp.dma_start(xa[:, slot, :, :].rearrange("p (s t) c -> p s (t c)", t=T),
                             x_rows[:, bass.ds(row, R), :]).then_inc(xa_load[slot], 16)

            def load_res(row, slot):
                sp.dma_start(ob[:, slot, :, :, :].rearrange("p s t c -> p s (t c)"),
                             x_rows[:, bass.ds(row, R), :]).then_inc(res_load[slot], 16)

            sp.wait_ge(zt_pe, 4 * (NB - 3))
            sp.wait_ge(zst_done, NB - 3)
            load_x(0, 0)
            load_x(R, 1)
            sp.wait_ge(soft_in, 2 * T)
            for m in range(2):
                load_res(m * R, m)

            def turn_x(t, b):
                sp.dma_start_transpose(xt[:, b, t, :, :], xs[:, b, t, :, :].rearrange("p s c -> p (s c)"))\
                  .then_inc(xt_turn[b][t], 16)

            sp.wait_ge(xs_const, 4)
            for m in range(2):
                if m == 0:
                    sp.wait_ge(xhi_done, 1)
                    sp.wait_ge(xlo_done, 1)
                    for t in range(T):
                        turn_x(t, 0)
                    load_x(2 * R, 0)

            def count(it, per, n):
                return per * it + n if isinstance(it, int) else sp.snap(it * per + n)

            def step(it, c):
                if c % 2 == 0 and exists(it, c, -1):
                    q = c - 1
                    f, a = q // 4, q % 4 // 2
                    wait(sp, glo_sb, it, PERIOD, q + 1)
                    sp.sem_inc(turn_next, 1)
                    sp.dma_start_transpose(
                        gt[:, f % 3, a, :, :, :].rearrange("p l s n -> p (l s) n"),
                        gh[:, f % 2, a, :, :, :].rearrange("p l s n -> p (l s n)")).then_inc(gt_turn[f % 2][a], 16)
                if c % 12 == 8 and exists(it, c, 16):
                    m = (c + 4) // PAIRS + 1
                    wait(sp, xlo_done, it, 2, m + 1)
                    sp.sem_inc(turn_next, 1)
                    for t in range(T):
                        turn_x(t, m % 2)
                    if exists(it, c, 16 + PERIOD):
                        load_x(count(it, 2 * R, (m + 2) * R), m % 2)
                if c % 12 == 9 and exists(it, c, -21):
                    n = (c - 21) // PAIRS
                    row, ended = count(it, 2 * R, n * R), count(it, 2 * T, T * (n + 1))
                    sp.wait_ge(fin_sb, ended)
                    sp.dma_start(out_rows[:, bass.ds(row, R), :],
                                 ob[:, n % 2, :, :, :].rearrange("p s t c -> p s (t c)"))\
                      .then_inc(out_store[n % 2], 16)
                if c % 12 == 11 and exists(it, c, 1) and exists(it, c, -23):
                    n = (c - 23) // PAIRS
                    row, stored = count(it, 2 * R, (n + 2) * R), count(it, 16, 16 * (n // 2 + 1))
                    sp.wait_ge(out_store[n % 2], stored)
                    load_res(row, n % 2)

            steps(sp, step)
            for b in range(2):
                sp.wait_ge(out_store[b], 16 * NG // 2)

        @block.gpsimd
        def _(pool):
            pool.memset(ident[:, :], 0.0).then_inc(consts, 1)
            pool.memset(drop_m[:, :], 0.0).then_inc(consts, 1)
            pool.memset(beta_sel[:, :], 0.0).then_inc(consts, 1)
            pool.memset(bias_sel[:, :], 0.0).then_inc(consts, 1)
            pool.wait_ge(consts, 4)
            pool.affine_select(out=ident[:, :], in_=ident[:, :], compare_op=ALU.not_equal, fill=1.0, base=0,
                               pattern=[[-1, P]], channel_multiplier=1).then_inc(consts, 1)
            pool.affine_select(out=drop_m[:, :], in_=drop_m[:, :], compare_op=ALU.not_equal, fill=-1.0,
                               base=-(C - 1), pattern=[[0, P]], channel_multiplier=1).then_inc(consts, 1)
            pool.wait_ge(consts, 6)
            pool.affine_select(out=drop_m[:, :], in_=drop_m[:, :], compare_op=ALU.not_equal, fill=1.0, base=0,
                               pattern=[[0, 2], [-1, C]], channel_multiplier=1).then_inc(consts, 1)
            pool.wait_ge(consts, 7)
            for c in (C - 1, 2 * C - 1):
                pool.memset(drop_m[:, c:c + 1], 0.0).then_inc(consts, 1)
                pool.memset(bias_sel[:, c:c + 1], 1.0).then_inc(consts, 1)
            pool.memset(ones_row[:, :], 1.0).then_inc(consts, 1)
            pool.memset(mean_m[:, :], 1.0 / P).then_inc(consts, 1)
            pool.memset(wzc[:, :], 0.0).then_inc(consts, 1)
            pool.memset(eps_c[:, :], EPS).then_inc(consts, 1)
            pool.memset(eps_z[:, :], CZ * EPS).then_inc(consts, 1)
            pool.memset(mhalf[:, :], -0.5).then_inc(consts, 1)
            pool.wait_ge(wmax_ready, 1)
            pool.partition_all_reduce(wmaxa[:, :], wmax[:, :], P, ABSMAX).then_inc(wmaxa_ready, 1)

            mean_b = gn_mean[:, :].unsqueeze(1).broadcast_to([P, R * T, C])
            rstd_b = gn_rstd[:, :].unsqueeze(1).broadcast_to([P, R * T, C])
            bo_b = bzo[:, H:H + C].unsqueeze(1).broadcast_to([P, R * T, C])
            lnm_b = ln_mean[:, :].unsqueeze(2).broadcast_to([P, R * T, C])
            lnr_b = ln_rstd[:, :].unsqueeze(2).broadcast_to([P, R * T, C])

            def shift(it, e):
                a = xa[:, e, :, :]
                wait(pool, xa_load[e], it, 16, 16)
                pool.tensor_tensor(a, a, mean_b, op=ALU.subtract).then_inc(ln_shifted, 1)

            def z_rstd(i, t, b):
                n = t * QT_LOOPS * ITER + b
                wait(pool, zst_done, i, ITER, n + 1)
                wait(pool, zrs_ready, i, ITER, n - 1)
                keys = bass.ds(i * (ITER * ZB) + b * ZB, ZB)
                pool.tensor_tensor(zvar[:, b % 2, :], zst[:, keys, 2], eps_z[:, :], op=ALU.add).then_inc(zvar_ready, 1)
                wait(pool, zvar_ready, i, ITER, n + 1)
                pool.tensor_tensor(zrs[:, keys], zvar[:, b % 2, :],
                                   mhalf[:, 0:ZB], op=ALU.pow).then_inc(zrs_ready, 1)

            pool.dma_start(mk[:, :], mask_rows[:, 0, :]).then_inc(mask_load, 16)
            for t in range(T):
                def scale(i, first, last, t=t):
                    if first and t:
                        pool.wait_ge(bk_sb, t * QT_LOOPS * ITER)
                        pool.wait_ge(zrs_ready, t * QT_LOOPS * ITER)
                        for half in range(2):
                            divide_std(pool, t - 1, half).then_inc(lg_scaled, 1)
                        pool.wait_ge(lg_scaled, 2 * t)
                    for b in range(ITER):
                        if last and b == BEFORE_X:
                            pool.wait_ge(zt_pe, 4 * (NB - 3))
                            pool.wait_ge(zst_done, NB - 3)
                            for e in range(2):
                                pool.memset(xs[:, e, :, :, C - 1:C], 1.0).then_inc(xs_const, 1)
                                pool.memset(xs[:, e, :, :, 2 * C - 1:2 * C], 0.0).then_inc(xs_const, 1)
                            pool.wait_ge(gn_ready, 2)
                            shift(0, 0)
                        if not last or b < BEFORE_X:
                            z_rstd(i, t, b)
                        if first and t and b in (2, 3):
                            half = b - 2
                            pool.wait_ge(esum_inv, 2 * (t - 1) + half + 1)
                            divide_sum(pool, t - 1, half).then_inc(soft_w, 1)
                            if half == 0:
                                pool.wait_ge(soft_in, 2 * t)
                                pool.dma_start(mk[:, :], mask_rows[:, t, :]).then_inc(mask_load, 16)

                passes(pool, t, scale)

            def normalise(it, e):
                a = xa[:, e, :, :]
                wait(pool, ln_shifted, it, 2, e + 1)
                pool.tensor_tensor(a, a, rstd_b, op=ALU.mult).then_inc(ln_scaled, 1)
                wait(pool, ln_mean_ok, it, 2, e + 1)
                pool.tensor_tensor(a, a, lnm_b, op=ALU.subtract).then_inc(ln_centred, 1)
                wait(pool, ln_var_ok, it, 2, e + 1)
                pool.tensor_tensor(ln_rstd[:, :], ln_var[:, :], mhalf[:, :], op=ALU.pow).then_inc(ln_rstd_ok, 1)
                wait(pool, ln_rstd_ok, it, 2, e + 1)
                pool.tensor_tensor(a, a, lnr_b, op=ALU.mult).then_inc(ln_normed, 1)
                wait(pool, xhi_done, it, 2, e + 1)
                lo = xs[:, e, :, :, C:2 * C - 1].rearrange("p t s c -> p s t c")
                hi = xs[:, e, :, :, 0:C - 1].rearrange("p t s c -> p s t c")
                pool.tensor_tensor(lo, a[:, :, 0:C - 1].rearrange("p (s t) c -> p s t c", t=T), hi,
                                   op=ALU.subtract).then_inc(xlo_done, 1)

            def residual(it, e):
                r = ob[:, e, :, :, :].rearrange("p s t c -> p (s t) c")
                wait(pool, res_load[e], it, 16, 16)
                pool.tensor_tensor(r, r, bo_b, op=ALU.add).then_inc(res_ready, 1)

            normalise(0, 0)
            shift(0, 1)
            normalise(0, 1)
            loop_start[0] = 1
            with pool.Fori(1, NG // 2) as it:
                for e in range(2):
                    shift(it, e)
                    normalise(it, e)
                    residual(it - 1, e)
            loop_start[0] = 0
            residual(NG // 2 - 1, 0)
            residual(NG // 2 - 1, 1)

        @block.scalar
        def _(act):
            def exponentials(t, half):
                act.wait_ge(soft_in, 2 * t + half + 1)
                for h in range(4 * half, 4 * half + 4):
                    act.activation(lg[:, t, h, :], lg[:, t, h, :], ACT.Exp, bias=nmax[:, h:h + 1],
                                   accum_out=esum[:, h:h + 1]).then_inc(soft_exp, 1)

            def weights_hi(t, half):
                for k in range(T):
                    w = (2 * t + half) * T + k
                    act.wait_ge(wt_pe, w + 1)
                    act.activation(wth[:, k, 4 * half:4 * half + 4, t * P:(t + 1) * P],
                                   ps_w[w % 2][:, :].rearrange("p (h q) -> p h q", h=4), ACT.Copy)\
                       .then_inc(wh_sb, 1)

            for t in range(T):
                def turn(i, first, last, t=t):
                    for b in range(ITER + 1):
                        n = t * QT_LOOPS * ITER + b
                        if b < ITER:
                            wait(act, lg_pe, i, ITER, n - 1)
                            for j in range(4):
                                wait(act, zt_pe, i, 4 * ITER, 4 * n + j + 1)
                                act.activation(ztr[:, b % 2, j, :], bank[j][:, :], ACT.Copy).then_inc(zt_sb, 1)
                        if b:
                            wait(act, lg_pe, i, ITER, n)
                            wait(act, bk_pe, i, ITER, n - 1)
                            act.activation(lraw[:, :], ps_lg[:, :], ACT.Copy).then_inc(lg_sb, 1)
                        if first and t:
                            if b in (3, 4):
                                exponentials(t - 1, b - 3)
                            if b == 6:
                                weights_hi(t - 1, 0)
                                weights_hi(t - 1, 1)
                        if last and b == 6:
                            act.wait_ge(gn_var, 1)
                            act.activation(gn[:, 5, :], gn[:, 4, :], ACT.Sqrt).then_inc(gn_std, 1)

                passes(act, t, turn)

            def square(m):
                act.activation(sq, xa[:, m % 2, :, :], ACT.Square).then_inc(ln_squared, 1)

            def store_hi(m):
                act.activation(xs[:, m % 2, :, :, 0:C - 1].rearrange("p t s c -> p s t c"),
                               xa[:, m % 2, :, 0:C - 1].rearrange("p (s t) c -> p s t c", t=T), ACT.Copy)\
                   .then_inc(xhi_done, 1)

            act.wait_ge(zlast_var, 1)
            act.activation(zvar, zvar, ACT.Sqrt).then_inc(zlast_std, 1)
            exponentials(T - 1, 0)
            act.wait_ge(ln_centred, 1)
            square(0)
            exponentials(T - 1, 1)
            weights_hi(T - 1, 0)
            act.wait_ge(ln_normed, 1)
            store_hi(0)
            weights_hi(T - 1, 1)

            def step(it, c):
                two = lambda off: (off % PERIOD) // PAIRS
                if exists(it, c, 12):
                    q = c + 12
                    t, sp_ = q % PAIRS // 4, q % 4
                    wait(act, v_pe, it, PERIOD, q + 1)
                    if q % PAIRS == 0:
                        wait(act, o_pe, it, PERIOD, q - PAIRS)
                    act.activation(vh[:, two(q), t, :, 2 * sp_:2 * sp_ + 2, :].rearrange("p h s c -> p s h c"),
                                   ps_v[q % 2][:, :].rearrange("p (s h c) -> p s h c", s=2, h=H), ACT.Copy)\
                       .then_inc(vh_sb, 1)
                if exists(it, c, 4):
                    q = c + 4
                    wait(act, g_pe, it, PERIOD, q + 1)
                    if q % 4 == 0:
                        wait(act, gated_sb, it, PERIOD, q - 4)
                    act.activation(gate[:, q // 4 % 2, 2 * (q % 4):2 * (q % 4) + 2, :]
                                   .rearrange("p s n -> p (s n)"), ps_g[:, :], ACT.Sigmoid,
                                   scale=wback[:, 1:2]).then_inc(g_sb, 1)
                if exists(it, c, 0):
                    q, f, hp = c, c // 4, c % 4
                    wait(act, gated_sb, it, PERIOD, q + 1)
                    if hp % 2 == 0:
                        wait(act, gt_turn[f % 2][hp // 2], it, 48, 16 * (f // 2))
                    act.activation(gh[:, f % 2, hp // 2, 0, :, hp % 2 * C:(hp % 2 + 1) * C],
                                   gated[:, q % 2, :, :], ACT.Copy).then_inc(ghi_sb, 1)
                m = ln_group(c, 10, 6)
                if m and exists(it, c, 22):
                    wait(act, ln_centred, it, 2, m + 1)
                    square(m)
                m = ln_group(c, 6, 1)
                if m and exists(it, c, 18):
                    wait(act, ln_normed, it, 2, m + 1)
                    for t in range(T):
                        wait(act, xt_turn[m % 2][t], it, 16, 16 * (m // 2))
                    store_hi(m)

            steps(act, step)

        @block.vector
        def _(dve):
            links = [0]

            def link(ins):
                ins.then_inc(dlink, 1)
                links[0] += 1
                dve.wait_ge(dlink, links[0])

            dve.wait_ge(par_load, 12 * 16)
            dve.wait_ge(consts, 17)
            dve.tensor_tensor(centre_m[:, :], ident[:, :], mean_m[:, :], op=ALU.subtract)
            dve.tensor_copy(beta_sel[:, C - 1:C], vec[0:C, 3:4])
            dve.tensor_copy(beta_sel[:, 2 * C - 1:2 * C], vec[0:C, 3:4])
            dve.tensor_scalar(wvg_g[:, :], wvg[:, :], vec[0:C, 2:3], None, ALU.mult)
            dve.tensor_scalar(wz_g[:, :], wz[:, :], vec[:, 0:1], None, ALU.mult)
            dve.tensor_scalar(beta_zb[:, :], mean_m[:, :], float(P), vec[:, 1:2], ALU.mult, ALU.mult)\
               .then_inc(prep_w, 1)
            dve.wait_ge(wprod, 1)
            dve.tensor_scalar(wzc[:, 0:H], bank[7][:, 0:H], float(CZ) ** 0.5, None, ALU.mult)
            dve.tensor_copy(bzo[:, :], bank[7][:, H:2 * H + C])
            link(dve.tensor_copy(wfull[:, :], bank[6][:, :]))
            for i in range(2):
                dve.tensor_reduce(wmax[:, i:i + 1], wfull[:, i * D:(i + 1) * D], axis=AX_X, op=ALU.max,
                                  apply_absolute_value=True)
            dve.tensor_reduce(wmax[:, 2:3], wo[:, :, :].rearrange("p a n -> p (a n)"), axis=AX_X, op=ALU.max,
                              apply_absolute_value=True).then_inc(wmax_ready, 1)
            dve.wait_ge(wmaxa_ready, 1)
            link(dve.tensor_scalar(wmaxa[:, :], wmaxa[:, :], 1e-30, None, ALU.max))
            link(dve.tensor_scalar(wpow[:, :].bitcast(I32), wmaxa[:, :].bitcast(I32), 0x7F800000, None,
                                   ALU.bitwise_and))
            link(dve.reciprocal(wscale[:, :], wpow[:, :]))
            dve.tensor_scalar(wback[:, :], wpow[:, :], 1.0 / W_TARGET, None, ALU.mult)
            link(dve.tensor_scalar(wscale[:, :], wscale[:, :], W_TARGET, None, ALU.mult))
            dve.tensor_tensor(oscale[:, :], wback[:, 0:1], wback[:, 2:3], op=ALU.mult)
            for i in range(2):
                dve.tensor_scalar(wvg_hi[:, i * D:(i + 1) * D], wfull[:, i * D:(i + 1) * D], wscale[:, i:i + 1],
                                  None, ALU.mult)
            link(dve.tensor_scalar(wo_hi[:, :, :], wo[:, :, :], wscale[:, 2:3], None, ALU.mult))
            for i in range(2):
                dve.scalar_tensor_tensor(wvg_lo[:, i * D:(i + 1) * D], wfull[:, i * D:(i + 1) * D],
                                         wscale[:, i:i + 1], wvg_hi[:, i * D:(i + 1) * D], ALU.mult, ALU.subtract)
            dve.scalar_tensor_tensor(wo_lo[:, :, :], wo[:, :, :], wscale[:, 2:3], wo_hi[:, :, :],
                                     ALU.mult, ALU.subtract).then_inc(w_ready, 1)

            def group_norm():
                cnt = 2 * NX
                dve.wait_ge(xst_done, NX)
                dve.wait_ge(zt_pe, 4 * (NB - 2))
                dve.wait_ge(zst_done, NB - 2)
                link(dve.tensor_reduce(gn[:, 0, :], xst3[:, :, :, 1], axis=AX_X, op=ALU.add))
                link(dve.tensor_scalar(gn[:, 0, :], gn[:, 0, :], 1.0 / cnt, None, ALU.mult))
                dve.tensor_copy(gn[:, 1, :], gn[:, 0, :]).then_inc(gn_part, 1)
                link(dve.tensor_tensor(tmp, xst3[:, :, :, 1], gn[:, 0, :].unsqueeze(2).broadcast_to([P, GRP, cnt]),
                                       op=ALU.subtract))
                link(dve.tensor_tensor(tmp, tmp, tmp, op=ALU.mult))
                link(dve.tensor_reduce(gn[:, 2, :], tmp, axis=AX_X, op=ALU.add))
                link(dve.tensor_reduce(gn[:, 3, :], xst3[:, :, :, 2], axis=AX_X, op=ALU.add))
                link(dve.scalar_tensor_tensor(gn[:, 2, :], gn[:, 2, :], float(XB), gn[:, 3, :], ALU.mult, ALU.add))
                dve.wait_ge(gn_mm, 1)
                for e in range(2):
                    dve.tensor_copy(gn_mean[:, :].rearrange("p (g e) -> p g e", e=2)[:, :, e], ps_w[1][:, 0:GRP])
                link(dve.tensor_tensor(gn[:, 3, :], gn[:, 0, :], ps_w[1][:, 0:GRP], op=ALU.subtract))
                link(dve.tensor_tensor(gn[:, 3, :], gn[:, 3, :], gn[:, 3, :], op=ALU.mult))
                dve.scalar_tensor_tensor(gn[:, 2, :], gn[:, 2, :], 1.0 / (cnt * XB), gn[:, 3, :],
                                         ALU.mult, ALU.add).then_inc(gn_part, 1)
                dve.wait_ge(gn_mm, 2)
                dve.tensor_scalar(gn[:, 4, :], ps_w[1][:, GRP:2 * GRP], EPS, None, ALU.add).then_inc(gn_var, 1)
                dve.wait_ge(gn_std, 1)
                link(dve.reciprocal(gn[:, 3, :], gn[:, 5, :]))
                for e in range(2):
                    dve.tensor_copy(gn_rstd[:, :].rearrange("p (g e) -> p g e", e=2)[:, :, e], gn[:, 3, :])\
                       .then_inc(gn_ready, 1)

            LO_AT = (19, 21, 23, 25, 27, 30)

            def mask_term(t):
                dve.wait_ge(mask_load, 16 * (t + 1))
                dve.tensor_scalar(mk[:, :], mk[:, :], -1.0, INF, ALU.add, ALU.mult).then_inc(mask_ready, 1)

            def biased(t, half):
                hs = slice(4 * half, 4 * half + 4)
                dve.wait_ge(mask_ready, t + 1)
                if t < T - 1:
                    dve.wait_ge(lg_scaled, 2 * t + half + 1)
                else:
                    dve.wait_ge(bk_sb, NB)
                    dve.wait_ge(zrs_ready, NB - ITER + BEFORE_X)
                    link(divide_std(dve, t, half))
                for h in range(4 * half, 4 * half + 4):
                    last = dve.scalar_tensor_tensor(lg[:, t, h, :], lg[:, t, h, :], bzo[:, h:h + 1], mk[:, :],
                                                    ALU.add, ALU.add)
                link(last)
                dve.tensor_reduce(nmax[:, hs], lg[:, t, hs, :], axis=AX_X, op=ALU.max, negate=True)\
                   .then_inc(soft_in, 1)

            def normalised(t, half):
                hs = slice(4 * half, 4 * half + 4)
                dve.wait_ge(soft_exp, H * t + 4 * half + 4)
                if t:
                    dve.wait_ge(soft_w, 2 * t)
                link(dve.reciprocal(einv[:, hs], esum[:, hs]))
                last = dve.tensor_scalar(einv[:, hs], einv[:, hs], W_SCALE, None, ALU.mult)
                last.then_inc(esum_inv, 1)
                if t == T - 1:
                    dve.wait_ge(esum_inv, 2 * t + half + 1)
                    divide_sum(dve, t, half).then_inc(soft_w, 1)

            def weights_lo(w):
                t, half, k = w // (2 * T), w // T % 2, w % T
                dve.wait_ge(wh_sb, w + 1)
                at = (slice(None), k, slice(4 * half, 4 * half + 4), slice(t * P, (t + 1) * P))
                dve.tensor_tensor(wtl[at], ps_w[w % 2][:, :].rearrange("p (h q) -> p h q", h=4), wth[at],
                                  op=ALU.subtract).then_inc(wl_sb, 1)

            for t in range(T):
                def measure(i, first, last, t=t):
                    def z_stats(b):
                        n = t * QT_LOOPS * ITER + b
                        wait(dve, z_load[b], i, 16, 16 * (n // ITER + 1))
                        if t:
                            wait(dve, zvar_ready, i, ITER, n - QT_LOOPS * ITER + 1)
                        for k in range(0, ZB, 2):
                            ins = dve.bn_stats(zst[:, bass.ds(i * (ITER * ZB) + (b * ZB + k), 2), :]
                                               .rearrange("p k s -> p (k s)"),
                                               z_buf[b][:, k:k + 2, :].rearrange("p k c -> p c k"))
                        ins.then_inc(zst_done, 1)

                    def keep_logits(b):
                        n = t * QT_LOOPS * ITER + b
                        wait(dve, bk_pe, i, ITER, n + 1)
                        dve.tensor_copy(
                            lg[:, t, :, bass.ds(i * (ITER * ZB) + b * ZB, ZB)]
                            .rearrange("p h (j k) -> p h j k", k=4),
                            ps_back[:, :].rearrange("p (k j h) -> p h j k", k=4, j=4)[:, 0:H, :, :])\
                           .then_inc(bk_sb, 1)

                    weave = first and t
                    for b in range(BEFORE_X):
                        if weave and b == 0:
                            mask_term(t - 1)
                        z_stats(b)
                        if b >= 2:
                            keep_logits(b - 2)
                        if weave and b in (1, 2):
                            biased(t - 1, b - 1)
                        if weave and b == 3:
                            normalised(t - 1, 0)
                    m = t * QT_LOOPS
                    wait(dve, xc_load, i, 16, 16 * (m + 1))
                    for g in range(GRP):
                        ins = dve.bn_stats(xst[:, g, bass.ds(i + m, 1), :].rearrange("p x s -> p (x s)"),
                                           xch[:, :, g, :])
                        if weave and g == 3:
                            normalised(t - 1, 1)
                        if g in (4, 10):
                            keep_logits(2 + g // 10)
                        if weave and g in LO_AT:
                            weights_lo((t - 1) * 2 * T + LO_AT.index(g))
                    ins.then_inc(xst_done, 1)
                    if last:
                        group_norm()
                    for b in range(BEFORE_X, ITER):
                        z_stats(b)
                        keep_logits(b)

                passes(dve, t, measure)

            def mean_of(m):
                dve.tensor_reduce(ln_sum[:, :], xa[:, m % 2, :, :], axis=AX_X, op=ALU.add).then_inc(ln_summed, 1)

            def variance_of(m):
                dve.tensor_reduce(ln_ssq[:, :], sq, axis=AX_X, op=ALU.add).then_inc(ln_ssummed, 1)

            def mean_out():
                dve.tensor_scalar(ln_mean[:, :], ln_sum[:, :], 1.0 / C, None, ALU.mult).then_inc(ln_mean_ok, 1)

            def variance_out():
                dve.tensor_scalar(ln_var[:, :], ln_ssq[:, :], 1.0 / C, EPS, ALU.mult, ALU.add)\
                   .then_inc(ln_var_ok, 1)

            mask_term(T - 1)
            dve.wait_ge(zrs_ready, NB - ITER + BEFORE_X)
            zlast = slice(N - (ITER - BEFORE_X) * ZB, N)
            dve.wait_ge(zst_done, NB)
            dve.tensor_scalar(zvar.rearrange("p b k -> p (b k)"), zst[:, zlast, 2], CZ * EPS, None, ALU.add)\
               .then_inc(zlast_var, 1)
            dve.wait_ge(zlast_std, 1)
            link(dve.reciprocal(zrs[:, zlast], zvar.rearrange("p b k -> p (b k)")))
            biased(T - 1, 0)
            dve.wait_ge(ln_scaled, 1)
            mean_of(0)
            dve.wait_ge(ln_summed, 1)
            mean_out()
            biased(T - 1, 1)
            normalised(T - 1, 0)
            dve.wait_ge(ln_squared, 1)
            variance_of(0)
            dve.wait_ge(ln_ssummed, 1)
            variance_out()
            normalised(T - 1, 1)
            for w in range(2 * T * (T - 1), 2 * T * T):
                weights_lo(w)

            def step(it, c):
                two = lambda off: (off % PERIOD) // PAIRS
                if exists(it, c, -1):
                    q, f, hp = c - 1, (c - 1) // 4, (c - 1) % 4
                    wait(dve, ghi_sb, it, PERIOD, q + 1)
                    cols = slice(hp % 2 * C, (hp % 2 + 1) * C)
                    dve.tensor_tensor(gh[:, f % 2, hp // 2, 1, :, cols], gated[:, q % 2, :, :],
                                      gh[:, f % 2, hp // 2, 0, :, cols], op=ALU.subtract).then_inc(glo_sb, 1)
                if exists(it, c, 12):
                    q = c + 12
                    t, sp_ = q % PAIRS // 4, q % 4
                    wait(dve, vh_sb, it, PERIOD, q + 1)
                    view = lambda v: v[:, two(q), t, :, 2 * sp_:2 * sp_ + 2, :].rearrange("p h s c -> p s h c")
                    dve.tensor_tensor(view(vl), ps_v[q % 2][:, :].rearrange("p (s h c) -> p s h c", s=2, h=H), view(vh),
                                      op=ALU.subtract).then_inc(vl_sb, 1)
                if exists(it, c, 0):
                    q, f, hp = c, c // 4, c % 4
                    wait(dve, o_pe, it, PERIOD, q + 1)
                    if hp == 0:
                        wait(dve, g_sb, it, PERIOD, q + 4)
                    wait(dve, glo_sb, it, PERIOD, q - 1)
                    heads = slice(2 * hp * (D // H), (2 * hp + 2) * (D // H))
                    dve.scalar_tensor_tensor(gated[:, q % 2, :, :],
                                             ps_o[q % 2][:, :].rearrange("p (s n) -> p s n", s=R), 1.0 / W_SCALE,
                                             gate[:, f % 2, :, heads], ALU.mult, ALU.mult).then_inc(gated_sb, 1)
                if c % 4 == 0 and exists(it, c, -12):
                    f = c // 4 - 3
                    t, n = f % T, f // T
                    wait(dve, p_pe, it, PERIOD, 4 * f + 4)
                    wait(dve, res_ready, it, 2, n + 1)
                    o = ob[:, n % 2, :, t, :]
                    dve.scalar_tensor_tensor(o, ps_p[f % 2][:, :].rearrange("p (s c) -> p s c", s=R), oscale[:, 0:1], o,
                                             ALU.mult, ALU.add).then_inc(fin_sb, 1)
                m = ln_group(c, 12, 10)
                if m and exists(it, c, 24):
                    wait(dve, ln_scaled, it, 2, m + 1)
                    mean_of(m)
                    wait(dve, ln_summed, it, 2, m + 1)
                    mean_out()
                m = ln_group(c, 9, 5)
                if m and exists(it, c, 21):
                    wait(dve, ln_squared, it, 2, m + 1)
                    variance_of(m)
                    wait(dve, ln_ssummed, it, 2, m + 1)
                    variance_out()

            steps(dve, step)

        @block.tensor
        def _(pe):
            mm = nc.tensor.matmul
            pe.wait_ge(consts, 17)
            pe.wait_ge(prep_w, 1)
            mm(bank[6][:, :], drop_m[:, :], wvg_g[:, :], start=True, stop=False)
            mm(bank[6][:, :], beta_sel[:, :], wvg[:, :], start=False, stop=False)
            mm(bank[6][:, :], bias_sel[:, :], bvg[:, :], start=False, stop=True)
            mm(bank[7][:, 0:H], centre_m[:, :], wz_g[:, :], start=True, stop=True)
            mm(bank[7][:, H:2 * H], beta_zb[:, :], wz[:, :], start=True, stop=False)
            mm(bank[7][:, H:2 * H], ones_row[:, :], brow[:, 0:H], start=False, stop=True)
            mm(bank[7][:, 2 * H:2 * H + C], ones_row[:, :], brow[:, H:H + C], start=True, stop=True)\
                .then_inc(wprod, 1)
            pe.wait_ge(w_ready, 1)

            def turn_weights(t, half):
                pe.wait_ge(soft_w, 2 * t + half + 1)
                for k in range(T):
                    w = (2 * t + half) * T + k
                    if w >= 2:
                        pe.wait_ge(wl_sb, w - 1)
                    for j in range(4):
                        blk = lg[:, t, 4 * half + j, :].rearrange("p (k t) -> p t k", t=T)[:, k, :]
                        last = nc.tensor.transpose(ps_w[w % 2][:, j * P:(j + 1) * P], blk, ident[:, :])
                    last.then_inc(wt_pe, 1)

            for t in range(T):
                def logits(i, first, last, t=t):
                    for b in range(ITER + 2):
                        n = t * QT_LOOPS * ITER + b
                        if b < ITER:
                            wait(pe, z_load[b], i, 16, 16 * (n // ITER + 1))
                            for j in range(4):
                                wait(pe, zt_sb, i, 4 * ITER, 4 * n + j - 3)
                                for k in range(4):
                                    ins = nc.tensor.transpose(bank[j][:, k * P:(k + 1) * P],
                                                               z_buf[b][:, 4 * j + k, :], ident[:, :])
                                ins.then_inc(zt_pe, 1)
                        if b >= 2:
                            wait(pe, lg_sb, i, ITER, n - 1)
                            wait(pe, bk_sb, i, ITER, n - 2)
                            for k in range(4):
                                ins = nc.tensor.transpose(ps_back[:, k * P:(k + 1) * P],
                                                           lraw[:, k * P:(k + 1) * P], ident[:, :])
                            ins.then_inc(bk_pe, 1)
                        if 1 <= b <= ITER:
                            wait(pe, zt_sb, i, 4 * ITER, 4 * n)
                            wait(pe, lg_sb, i, ITER, n - 1)
                            for j in range(4):
                                ins = mm(ps_lg[32 * j:32 * j + 32, :], wzc[:, :], ztr[:, (b - 1) % 2, j, :],
                                          start=True, stop=True)
                            ins.then_inc(lg_pe, 1)
                        if first and t and b == 6:
                            turn_weights(t - 1, 0)
                            turn_weights(t - 1, 1)
                        if last and b == 6:
                            pe.wait_ge(wl_sb, 2 * T * (T - 1))
                            for part, src in enumerate((1, 2)):
                                pe.wait_ge(gn_part, part + 1)
                                mm(ps_w[1][:, part * GRP:(part + 1) * GRP], mean_m[:, :], gn[:, src, :], start=True, stop=True)\
                                    .then_inc(gn_mm, 1)

                passes(pe, t, logits)
            pe.wait_ge(gn_ready, 2)
            turn_weights(T - 1, 0)
            turn_weights(T - 1, 1)

            pe.wait_ge(bk_sb, NB)

            def step(it, c):
                two = lambda off: (off % PERIOD) // PAIRS

                def average(hh):
                    q, t, h = c, c % PAIRS // 4, 2 * (c % 4) + hh
                    for k in range(T):
                        w_hi, w_lo = wth[:, k, h, t * P:(t + 1) * P], wtl[:, k, h, t * P:(t + 1) * P]
                        v_hi, v_lo = vh[:, two(q), k, h, :, :], vl[:, two(q), k, h, :, :]
                        o = ps_o[q % 2][:, :].rearrange("p (s h c) -> p h s c", s=R, h=2)[:, hh, :, :]
                        mm(o, w_hi, v_hi, start=k == 0, stop=False)
                        mm(o, w_hi, v_lo, start=False, stop=False)
                        last = mm(o, w_lo, v_hi, start=False, stop=k == T - 1)
                    if hh == 1:
                        last.then_inc(o_pe, 1)

                def project(it, q, ps, done, free, buffers, off):
                    if not exists(it, q, 0):
                        return
                    if q % 4 == 0:
                        wait(pe, xt_turn[two(q)][q % PAIRS // 4], it, 16, 16 * (q // PERIOD + 1))
                    wait(pe, free, it, PERIOD, q - buffers + 1)
                    for s in range(2):
                        x_t = xt[:, two(q), q % PAIRS // 4, 2 * (q % 4) + s, :]
                        mm(ps[:, s * D:(s + 1) * D], x_t, wvg_hi[:, off:off + D], start=True, stop=False)
                        last = mm(ps[:, s * D:(s + 1) * D], x_t, wvg_lo[:, off:off + D], start=False, stop=True)
                    last.then_inc(done, 1)

                if exists(it, c, 0):
                    wait(pe, gated_sb, it, PERIOD, c - 1)
                    if c % PAIRS == 0:
                        wait(pe, vh_sb, it, PERIOD, c + PAIRS)
                        wait(pe, vl_sb, it, PERIOD, c + PAIRS)
                    average(0)
                project(it, c + 12, ps_v[c % 2], v_pe, vl_sb, 2, 0)
                project(it, c + 4, ps_g, g_pe, g_sb, 1, D)
                if exists(it, c, 0):
                    average(1)
                if exists(it, c, -8):
                    q, f = c - 8, (c - 8) // 4
                    if q % 4 == 0:
                        for a in range(2):
                            wait(pe, gt_turn[f % 2][a], it, 48, 16 * (f // 2 + 1))
                        wait(pe, fin_sb, it, 2 * T, f - 1)
                    for row in range(2 * (q % 4), 2 * (q % 4) + 2):
                        o = ps_p[f % 2][:, row * C:(row + 1) * C]
                        for a in range(2):
                            g_hi, g_lo = gt[:, f % 3, a, 0, row, :], gt[:, f % 3, a, 1, row, :]
                            mm(o, g_hi, wo_hi[:, a, :], start=a == 0, stop=False)
                            mm(o, g_hi, wo_lo[:, a, :], start=False, stop=False)
                            last = mm(o, g_lo, wo_hi[:, a, :], start=False, stop=a == 1)
                    last.then_inc(p_pe, 1)

            steps(pe, step)


_INS = ["x"] + ["L0_conv_" + n for n in ("z", "mask", "gamma_m", "beta_m", "gamma_z", "beta_z", "w_z", "b_z",
                                         "w_v", "b_v", "w_g", "b_g", "w_o", "b_o")]


def kernel(**inputs):
    import numpy as np
    import concourse.bacc as bacc
    from concourse.bass_utils import run_bass_kernel_spmd

    nc = bacc.Bacc("TRN2", target_bir_lowering=False, num_devices=1)
    arrays, args = {}, []
    for name in _INS:
        a = np.ascontiguousarray(inputs[name])
        arrays[f"in_{name}"] = a
        args.append(nc.dram_tensor(f"in_{name}", a.shape, mybir.dt.from_np(a.dtype), kind="ExternalInput").ap())
    args.append(nc.dram_tensor("out", arrays["in_x"].shape, F32, kind="ExternalOutput").ap())
    pair_weighted(nc, *args)
    return run_bass_kernel_spmd(nc, [arrays], core_ids=[0]).results[0]["out"]
```
